# Optimizing a Trainium2 kernel written in Bass

```python
import numpy as np
import jax
import jax.numpy as jnp

def _softmax(x, axis=-1):
    return jax.nn.softmax(x, axis=axis)

def _gelu(x):
    return jax.nn.gelu(x, approximate=True)

def _silu(x):
    return jax.nn.silu(x)

def _sigmoid(x):
    return jax.nn.sigmoid(x)

def _layernorm(x, axis=-1, eps=1e-05):
    m = jnp.mean(x, axis=axis, keepdims=True)
    v = jnp.var(x, axis=axis, keepdims=True)
    return (x - m) / jnp.sqrt(v + eps)

def _scatter_add(tgt, idx, src, axis=0):
    return tgt.at[idx].add(src)

def _segment_sum(src, seg, n):
    return jax.ops.segment_sum(src, seg, n)
kernel_name = 'mk_seq_preln_d1_jaxref_r4_ad0c8f'

def setup_inputs(seed: int=0):
    np.random.seed(seed)
    _w = jnp.asarray

    def _L0_attn_setup():
        import jax, jax.numpy as jnp
        import numpy as np
        DT_RANK = 64
        D_STATE = 16

        def _selective_scan(u, delta, A, Bm, Cm):
            deltaA = jnp.exp(delta[..., None] * A[None, None])
            deltaB_u = delta[..., None] * Bm[:, :, None, :] * u[..., None]

            def step(h, inp):
                dA, dBu, c = inp
                h = dA * h + dBu
                y = jnp.einsum('bdn,bn->bd', h, c)
                return (h, y)
            b, l, d = u.shape
            h0 = jnp.zeros((b, d, A.shape[1]), dtype=u.dtype)
            xs = (jnp.moveaxis(deltaA, 1, 0), jnp.moveaxis(deltaB_u, 1, 0), jnp.moveaxis(Cm, 1, 0))
            _, ys = jax.lax.scan(step, h0, xs)
            return jnp.moveaxis(ys, 0, 1)
        key = jax.random.key(seed)
        ks = jax.random.split(key, 6)
        B, L, Di = (2, 512, 512)
        x = jax.random.normal(ks[0], (B, L, Di), dtype=jnp.float32)
        W_xproj = jax.random.normal(ks[1], (DT_RANK + 2 * D_STATE, Di), dtype=jnp.float32) * Di ** (-0.5)
        W_dt = jax.random.uniform(ks[2], (Di, DT_RANK), dtype=jnp.float32, minval=-DT_RANK ** (-0.5), maxval=DT_RANK ** (-0.5))
        dt = jnp.exp(jax.random.uniform(ks[3], (Di,), dtype=jnp.float32) * (np.log(0.1) - np.log(0.001)) + np.log(0.001))
        b_dt = dt + jnp.log(-jnp.expm1(-dt))
        A_log = jnp.log(jnp.broadcast_to(jnp.arange(1, D_STATE + 1, dtype=jnp.float32), (Di, D_STATE)))
        D_param = jnp.ones((Di,), dtype=jnp.float32)
        return {'x': x, 'W_xproj': W_xproj, 'W_dt': W_dt, 'b_dt': b_dt, 'A_log': A_log, 'D_param': D_param}
    _L0_attn_in = _L0_attn_setup()

    def _L0_ffn_setup():
        import jax, jax.numpy as jnp
        import numpy as np
        EPS = 1e-06
        Q_B = 128.0

        def layer_norm(x):
            mean = jnp.mean(x, axis=-1, keepdims=True)
            var = jnp.var(x, axis=-1, keepdims=True)
            return (x - mean) / jnp.sqrt(var + EPS)

        def absmax_quant(x):
            gamma = jnp.max(jnp.abs(x), axis=-1, keepdims=True)
            x_hat = jnp.clip(x * Q_B / gamma, -Q_B + EPS, Q_B - EPS)
            return x_hat * gamma / Q_B

        def ternarize_weights(w):
            gamma = jnp.mean(jnp.abs(w))
            return jnp.sign(jnp.round(w / (gamma + EPS))) * gamma

        def bitlinear(x, w):
            xn = layer_norm(x)
            x_hat = xn + jax.lax.stop_gradient(absmax_quant(xn) - xn)
            w_hat = w + jax.lax.stop_gradient(ternarize_weights(w) - w)
            return jnp.einsum('bsd,od->bso', x_hat, w_hat)
        key = jax.random.key(seed)
        k1, k2, k3 = jax.random.split(key, 3)
        B, S, D = (4, 512, 512)
        x = jax.random.normal(k1, (B, S, D), dtype=jnp.float32)
        w_fc = jax.random.normal(k2, (4 * D, D), dtype=jnp.float32) / np.sqrt(D)
        w_proj = jax.random.normal(k3, (D, 4 * D), dtype=jnp.float32) / np.sqrt(4 * D)
        return {'x': x, 'w_fc': w_fc, 'w_proj': w_proj}
    _L0_ffn_in = _L0_ffn_setup()
    _d = {'L0_attn_x': _L0_attn_in['x'], 'L0_attn_W_xproj': _L0_attn_in['W_xproj'], 'L0_attn_W_dt': _L0_attn_in['W_dt'], 'L0_attn_b_dt': _L0_attn_in['b_dt'], 'L0_attn_A_log': _L0_attn_in['A_log'], 'L0_attn_D_param': _L0_attn_in['D_param'], 'L0_ffn_w_fc': _L0_ffn_in['w_fc'], 'L0_ffn_w_proj': _L0_ffn_in['w_proj']}
    _x0 = _d['L0_attn_x']
    _d['L0_attn_x'] = jax.random.normal(jax.random.fold_in(jax.random.key(seed), 1), (4, 1024, 512), dtype=_x0.dtype)
    del _x0
    return _d

def reference(L0_attn_x, L0_attn_W_xproj, L0_attn_W_dt, L0_attn_b_dt, L0_attn_A_log, L0_attn_D_param, L0_ffn_w_fc, L0_ffn_w_proj):

    def _L0_attn_ref(x, W_xproj, W_dt, b_dt, A_log, D_param):
        import jax, jax.numpy as jnp
        import numpy as np
        DT_RANK = 64
        D_STATE = 16

        def _selective_scan(u, delta, A, Bm, Cm):
            deltaA = jnp.exp(delta[..., None] * A[None, None])
            deltaB_u = delta[..., None] * Bm[:, :, None, :] * u[..., None]

            def step(h, inp):
                dA, dBu, c = inp
                h = dA * h + dBu
                y = jnp.einsum('bdn,bn->bd', h, c)
                return (h, y)
            b, l, d = u.shape
            h0 = jnp.zeros((b, d, A.shape[1]), dtype=u.dtype)
            xs = (jnp.moveaxis(deltaA, 1, 0), jnp.moveaxis(deltaB_u, 1, 0), jnp.moveaxis(Cm, 1, 0))
            _, ys = jax.lax.scan(step, h0, xs)
            return jnp.moveaxis(ys, 0, 1)
        x_dbl = jnp.einsum('bld,ed->ble', x, W_xproj)
        dlt = x_dbl[..., :DT_RANK]
        Bm = x_dbl[..., DT_RANK:DT_RANK + D_STATE]
        Cm = x_dbl[..., DT_RANK + D_STATE:]
        delta = jax.nn.softplus(jnp.einsum('blr,dr->bld', dlt, W_dt) + b_dt)
        A = -jnp.exp(A_log.astype(jnp.float32))
        y = _selective_scan(x, delta, A, Bm, Cm)
        return y + x * D_param[None, None, :]

    def _L0_ffn_ref(x, w_fc, w_proj):
        import jax, jax.numpy as jnp
        import numpy as np
        EPS = 1e-06
        Q_B = 128.0

        def layer_norm(x):
            mean = jnp.mean(x, axis=-1, keepdims=True)
            var = jnp.var(x, axis=-1, keepdims=True)
            return (x - mean) / jnp.sqrt(var + EPS)

        def absmax_quant(x):
            gamma = jnp.max(jnp.abs(x), axis=-1, keepdims=True)
            x_hat = jnp.clip(x * Q_B / gamma, -Q_B + EPS, Q_B - EPS)
            return x_hat * gamma / Q_B

        def ternarize_weights(w):
            gamma = jnp.mean(jnp.abs(w))
            return jnp.sign(jnp.round(w / (gamma + EPS))) * gamma

        def bitlinear(x, w):
            xn = layer_norm(x)
            x_hat = xn + jax.lax.stop_gradient(absmax_quant(xn) - xn)
            w_hat = w + jax.lax.stop_gradient(ternarize_weights(w) - w)
            return jnp.einsum('bsd,od->bso', x_hat, w_hat)
        h = bitlinear(x, w_fc)
        h = jax.nn.gelu(h, approximate=False)
        return bitlinear(h, w_proj)
    x = L0_attn_x
    x = x + _L0_attn_ref(_layernorm(x, axis=-1), L0_attn_W_xproj, L0_attn_W_dt, L0_attn_b_dt, L0_attn_A_log, L0_attn_D_param)
    x = x + _L0_ffn_ref(_layernorm(x, axis=-1), L0_ffn_w_fc, L0_ffn_w_proj)
    return x

_drawn_inputs = setup_inputs


def setup_inputs(seed=0):
    import zlib

    import numpy as np

    out = dict(_drawn_inputs(seed))
    spreads = {'L0_attn_D_param': (1.0, 0.2)}
    factors = {}
    for name, (base, spread) in spreads.items():
        noise = np.random.default_rng([zlib.crc32(name.encode()), seed]).standard_normal(out[name].shape)
        drawn = base * np.exp(spread * noise) if base else spread * noise
        out[name] = jnp.asarray(drawn.astype(out[name].dtype))
    for name, factor in factors.items():
        out[name] = (out[name] * factor).astype(out[name].dtype)
    return out
```

```python
from contextlib import ExitStack

import concourse.bass as bass
from concourse import mybir

ALU = mybir.AluOpType
ACT = mybir.ActivationFunctionType
AX = mybir.AxisListType
F32 = mybir.dt.float32
F16 = mybir.dt.float16

P = 128
LN_EPS = 1e-5
BIT_EPS = 1e-6
QB = 128.0


def build(nc, x, wx_t, wdt_t, b_dt, a_log, d_param, w1_t, w2_t, out):
    B, L, D = x.shape
    NS = a_log.shape[2]
    R = wdt_t.shape[0]
    F = w1_t.shape[1]
    ND = D // P
    CH = 512
    NT = CH // P
    HALVES = L // CH
    STEPS = NS * ND
    FC = F // P
    NB = F // 512
    TILES = B * L // P
    XRING = 4

    xc = x.rearrange("b l d -> (b l) d").rearrange("(c a p) d -> p c a d", p=P, a=NT)
    oc = out.rearrange("b l d -> (b l) d").rearrange("(i p) d -> p i d", p=P)
    x1_dram = nc.dram_tensor("x1_dram", (B * L, D), F32).ap()
    x1c = x1_dram.rearrange("(c a p) d -> p c a d", p=P, a=NT)
    x1i = x1_dram.rearrange("(i p) d -> p i d", p=P)
    c_dram = nc.dram_tensor("c_dram", (B * HALVES, NS, CH), F32).ap()

    with ExitStack() as ctx:
        def sb(name, shape, dt=F32):
            return ctx.enter_context(nc.sbuf_tensor(name, shape, dt))

        def ps(name, shape, dt=F32):
            return ctx.enter_context(nc.psum_tensor(name, shape, dt))

        def sem(name):
            return ctx.enter_context(nc.semaphore(name))

        ident = sb("ident", [P, P])
        ones = sb("ones", [P, P])
        diag_d = sb("diag_d", [P, ND, P])
        wx = sb("wx", [P, ND, R + 2 * NS])
        wdt = sb("wdt", [R, D])
        bdt = sb("bdt", [P, ND])
        dpar = sb("dpar", [P, ND])
        neg_a = sb("neg_a", [P, ND, NS])
        w1 = sb("w1", [P, ND, F], F16)
        w2 = sb("w2", [P, FC, D], F16)
        wsum = sb("wsum", [P, 2])
        gam = sb("gam", [P, 2])
        thr = sb("thr", [P, 2])
        nthr = sb("nthr", [P, 2])
        mhalf = sb("mhalf", [P, 4])
        ln_eps = sb("ln_eps", [P, 4])
        bit_eps = sb("bit_eps", [P, 1])
        spare = sb("spare", [P, 1])
        xin = sb("xin", [P, 2, NT, D])
        s1 = sb("s1", [P, NT * D])
        ut = sb("ut", [P, ND, CH])
        delta = sb("delta", [P, 2, ND, CH])
        dut = sb("dut", [P, 2, NT, D])
        s2 = [dut[:, k].rearrange("p a d -> p (a d)") for k in range(2)]
        dc = sb("dc", [R + NS, CH])
        bt = sb("bt", [P, 2, NT, NS])
        bs = sb("bs", [P, 2, NT, D])
        da = sb("da", [P, 4, CH])
        hh = sb("hh", [P, 4, CH])
        pp = sb("pp", [P, 2, CH])
        hst = sb("hst", [P, STEPS])
        st6 = sb("st6", [P, NT, 6])
        mv = sb("mv", [P, NT, 2])
        rs = sb("rs", [P, NT])
        cb = sb("cb", [P, 2, NS * CH])
        w1_raw = cb[:, 0, :]
        w2_raw = cb[:, 1, :]

        y = ps("y", [P, NT, 512])
        dbu = ps("dbu", [P, 2, 512])
        aux = ps("aux", [P, 2, 512])

        w_in = sem("w_in")
        x_in = [sem(f"x_in{k}") for k in range(2)]
        raw_in = sem("raw_in")
        const_ready = sem("const_ready")
        id_ready = sem("id_ready")
        prep = sem("prep")
        abs_done = sem("abs_done")
        gam_psum = sem("gam_psum")
        gam_ready = sem("gam_ready")
        tern_done = sem("tern_done")
        mv_ready = sem("mv_ready")
        bn_ready = sem("bn_ready")
        ve_ready = sem("ve_ready")
        rs_ready = sem("rs_ready")
        u_ready = sem("u_ready")
        aux_full = sem("aux_full")
        aux_free = sem("aux_free")
        ut_ready = sem("ut_ready")
        dc_ready = sem("dc_ready")
        c_stored = sem("c_stored")
        cb_in = [sem(f"cb_in{k}") for k in range(2)]
        z_ready = sem("z_ready")
        absz_ready = sem("absz_ready")
        e_ready = sem("e_ready")
        l_ready = sem("l_ready")
        dchain = sem("dchain")
        du_ready = sem("du_ready")
        dut_ready = sem("dut_ready")
        skip_done = sem("skip_done")
        bs_ready = sem("bs_ready")
        btr_done = sem("btr_done")
        exp_ready = sem("exp_ready")
        scan_done = sem("scan_done")
        prod_done = sem("prod_done")
        rtr_done = sem("rtr_done")
        y_done = sem("y_done")
        x1_added = sem("x1_added")
        x1_out = sem("x1_out")
        state_saved = sem("state_saved")

        AUXN = 14
        BTR0, SCAN0, PROD0, RTR0, AUX0 = 8, 4, 4, 2, 2

        def chunk(b, h):
            return b * HALVES + h

        def carry_wait(value):
            if not isinstance(value, int):
                nc.vector.tensor_copy(spare[:, :], ones[:, 0:1])

        def batches(eng, batch):
            with eng.Fori(0, B - 1) as b:
                batch(b, True)
            batch(B - 1, False)

        with nc.Block() as block:
            @block.sync
            def _(sp):
                sp.dma_start(xin[:, 0], xc[:, 0]).then_inc(x_in[0], 16)
                sp.dma_start(wx[:, :, :], wx_t.rearrange("(a p) e -> p a e", p=P)).then_inc(w_in, 16)
                sp.dma_start(wdt[:, :], wdt_t).then_inc(w_in, 16)
                sp.dma_start(bdt[:, :], b_dt).then_inc(w_in, 16)
                sp.dma_start(dpar[:, :], d_param).then_inc(w_in, 16)
                sp.dma_start(neg_a[:, :, :], a_log).then_inc(w_in, 16)
                sp.dma_start(w1_raw, w1_t.rearrange("(a p) f -> p a f", p=P)).then_inc(raw_in, 16)
                sp.dma_start(w2_raw, w2_t.rearrange("(a p) f -> p a f", p=P)).then_inc(raw_in, 16)
                sp.dma_start(xin[:, 1], xc[:, 1]).then_inc(x_in[1], 16)

                def spread_c(b, h):
                    c = chunk(b, h)
                    sp.wait_ge(dc_ready, c + 1)
                    sp.dma_start(c_dram[bass.ds(c, 1)].rearrange("o n t -> (o n) t"), dc[R:R + NS, :]).then_inc(c_stored, 16)
                    sp.wait_ge(c_stored, c * 16 + 16)
                    if isinstance(b, int) and b == 0:
                        sp.wait_ge(tern_done, 2)
                    else:
                        sp.wait_ge(prod_done, c * STEPS + (PROD0 - STEPS))
                    sp.dma_start(cb[:, h, :], c_dram[bass.ds(c, 1)].rearrange("o n t -> (o n t)").partition_broadcast(P)).then_inc(cb_in[h], 16)

                spread_c(0, 0)

                def batch(b, more):
                    for h in range(HALVES):
                        c = chunk(b, h)
                        if h + 1 < HALVES:
                            spread_c(b, h + 1)
                        elif more:
                            spread_c(b + 1, 0)
                        sp.wait_ge(x1_added, c + 2)
                        sp.dma_start(x1c[:, bass.ds(c, 1)], xin[:, h:h + 1]).then_inc(x1_out, 16)
                        if more:
                            sp.wait_ge(x1_out, c * 16 + 16)
                            sp.dma_start(xin[:, h:h + 1], xc[:, bass.ds(c + 2, 1)]).then_inc(x_in[h], 16)

                batches(sp, batch)
                sp.wait_ge(x1_out, 16 * B * HALVES)

            @block.gpsimd
            def _(pool):
                nc.gpsimd.memset(ident[:, :], 0.0).then_inc(id_ready, 1)
                nc.gpsimd.memset(ones[:, :], 1.0).then_inc(id_ready, 1)
                nc.gpsimd.memset(mhalf[:, :], -0.5).then_inc(const_ready, 1)
                nc.gpsimd.memset(ln_eps[:, :], LN_EPS).then_inc(const_ready, 1)
                nc.gpsimd.memset(bit_eps[:, :], BIT_EPS).then_inc(const_ready, 1)
                pool.wait_ge(id_ready, 2)
                nc.gpsimd.affine_select(out=ident[:, :], in_=ident[:, :], compare_op=ALU.not_equal, fill=1.0,
                                        base=0, pattern=[[-1, P]], channel_multiplier=1).then_inc(id_ready, 1)
                pool.wait_ge(const_ready, 3)

                def rstd(c):
                    pool.wait_ge(mv_ready, c + 1)
                    nc.gpsimd.tensor_tensor(rs[:, :], mv[:, :, 1], ln_eps[:, :], ALU.add).then_inc(ve_ready, 1)
                    pool.wait_ge(ve_ready, c + 1)
                    nc.gpsimd.tensor_tensor(rs[:, :], rs[:, :], mhalf[:, :], ALU.pow).then_inc(rs_ready, 1)

                def du(c, h):
                    pool.wait_ge(dchain, c * 4 + 4)
                    nc.gpsimd.tensor_tensor(s1[:, :], delta[:, h].rearrange("p a t -> p (a t)"),
                                            ut[:, :, :].rearrange("p a t -> p (a t)"), ALU.mult).then_inc(du_ready, 1)

                rstd(0)
                du(0, 0)
                pool.sem_inc(prod_done, PROD0)

                def batch(b, more):
                    for h in range(HALVES):
                        c = chunk(b, h)
                        nxt = h + 1 < HALVES or more
                        pool.wait_ge(cb_in[h], b * 16 + 16)
                        for s in range(STEPS):
                            if nxt and s == 7:
                                rstd(c + 1)
                            if nxt and s == 50:
                                du(c + 1, 1 - h)
                            n = s // ND
                            pool.wait_ge(scan_done, c * STEPS + (SCAN0 + s + 1))
                            if h + 1 < HALVES:
                                nc.gpsimd.tensor_tensor(hst[:, s:s + 1], hh[:, s % 4, CH - 1:CH], ones[:, 0:1],
                                                        ALU.mult).then_inc(state_saved, 1)
                            pool.wait_ge(rtr_done, c * STEPS + (s + 1))
                            nc.gpsimd.tensor_tensor(pp[:, s % 2], hh[:, s % 4], cb[:, h, n * CH:(n + 1) * CH],
                                                    ALU.mult).then_inc(prod_done, 1)

                batches(pool, batch)

            @block.scalar
            def _(act):
                act.wait_ge(w_in, 5 * 16)
                nc.scalar.activation(neg_a[:, :, :], neg_a[:, :, :], ACT.Exp).then_inc(prep, 1)
                act.wait_ge(raw_in, 32)
                nc.scalar.activation(w1[:, :, :].rearrange("p a f -> p (a f)"), w1_raw, ACT.Abs,
                                     accum_out=wsum[:, 0:1]).then_inc(abs_done, 1)
                act.sem_inc(aux_free, AUX0)

                def evac(k, dst, src, ready, **kw):
                    act.wait_ge(aux_full, k + 1)
                    nc.scalar.activation(dst, src, ACT.Identity, **kw).then_inc(aux_free, 1)

                def chained(c, k):
                    act.wait_ge(aux_free, c * AUXN + (AUX0 + k))

                def evac_ut(c):
                    act.wait_ge(skip_done, c + 1)
                    for a in range(ND):
                        act.wait_ge(aux_full, c * AUXN + (a + 1))
                        nc.scalar.activation(ut[:, a], aux[:, a % 2], ACT.Copy).then_inc(aux_free, 1)

                def evac_proj(c, h):
                    act.wait_ge(aux_full, c * AUXN + 5)
                    if not (isinstance(c, int) and c == 0):
                        act.wait_ge(c_stored, c * 16)
                    nc.scalar.activation(dc[:, :], aux[0:R + NS, 0], ACT.Copy).then_inc(aux_free, 1)
                    act.wait_ge(aux_free, c * AUXN + (AUX0 + 5))
                    act.sem_inc(dc_ready, 1)
                    act.wait_ge(aux_full, c * AUXN + 6)
                    nc.scalar.activation(bt[:, h], aux[:, 1, 0:NT * NS].rearrange("p (a n) -> p a n", a=NT),
                                         ACT.Copy).then_inc(aux_free, 1)

                def evac_z(c, h):
                    for a in range(ND):
                        act.wait_ge(aux_full, c * AUXN + (7 + a))
                        nc.scalar.activation(delta[:, h, a], aux[:, a % 2], ACT.Identity,
                                             bias=bdt[:, a:a + 1]).then_inc(aux_free, 1)

                def softplus_parts(c, h):
                    act.wait_ge(aux_free, c * AUXN + (AUX0 + 10))
                    nc.scalar.activation(s2[h], delta[:, h].rearrange("p a t -> p (a t)"), ACT.Abs).then_inc(absz_ready, 1)
                    act.wait_ge(absz_ready, c + 1)
                    nc.scalar.activation(s1[:, :], s2[h], ACT.Exp, scale=-1.0).then_inc(e_ready, 1)
                    act.wait_ge(e_ready, c + 1)
                    nc.scalar.activation(s2[h], s1[:, :], ACT.Ln, bias=1.0).then_inc(l_ready, 1)

                def evac_dut(c, h):
                    for a in range(NT):
                        act.wait_ge(aux_full, c * AUXN + (11 + a))
                        nc.scalar.activation(dut[:, h, a], aux[:, a % 2], ACT.Copy).then_inc(aux_free, 1)

                evac_ut(0)
                evac_proj(0, 0)
                evac_z(0, 0)
                softplus_parts(0, 0)
                evac_dut(0, 0)

                def batch(b, more):
                    for h in range(HALVES):
                        c = chunk(b, h)
                        nxt = h + 1 < HALVES or more
                        act.wait_ge(aux_free, c * AUXN + (AUX0 + AUXN))
                        for s in range(STEPS):
                            n, a = divmod(s, ND)
                            if nxt and s == 16:
                                evac_ut(c + 1)
                            if nxt and s == 24:
                                evac_proj(c + 1, 1 - h)
                            if nxt and s == 30:
                                evac_z(c + 1, 1 - h)
                            if nxt and s == 38:
                                softplus_parts(c + 1, 1 - h)
                            if nxt and s == 58:
                                evac_dut(c + 1, 1 - h)
                            if a == 0:
                                act.wait_ge(btr_done, c * STEPS + (s + BTR0 - 4))
                                for t in range(NT):
                                    i = nc.scalar.activation(bs[:, n % 2, t], dut[:, h, t], ACT.Copy,
                                                             scale=bt[:, h, t, n:n + 1])
                                i.then_inc(bs_ready, 1)
                            act.wait_ge(scan_done, c * STEPS + (s + 1))
                            nc.scalar.activation(da[:, s % 4], delta[:, h, a], ACT.Exp,
                                                 scale=neg_a[:, a, n:n + 1]).then_inc(exp_ready, 1)

                act.wait_ge(prep, 2)
                batches(act, batch)

            @block.tensor
            def _(pe):
                pe.wait_ge(id_ready, 3)
                pe.wait_ge(w_in, 5 * 16)
                pe.wait_ge(abs_done, 2)
                nc.tensor.matmul(y[:, 0, 0:2], ones[:, :], wsum[:, :], start=True, stop=True).then_inc(gam_psum, 1)
                pe.sem_inc(rtr_done, RTR0)
                pe.sem_inc(btr_done, BTR0)
                pe.sem_inc(skip_done, 1)

                def make_ut(c):
                    pe.wait_ge(u_ready, c + 1)
                    for a in range(ND):
                        pe.wait_ge(aux_free, c * AUXN + (a + 1))
                        for t in range(NT):
                            i = nc.tensor.transpose(aux[:, a % 2, t * P:(t + 1) * P],
                                                    s1[:, t * D + a * P:t * D + (a + 1) * P], ident[:, :])
                        i.then_inc(aux_full, 1)

                def project(c):
                    pe.wait_ge(aux_free, c * AUXN + (AUX0 + 4))
                    for a in range(ND):
                        i = nc.tensor.matmul(aux[0:R + NS, 0], wx[:, a, 0:R + NS], ut[:, a], start=(a == 0), stop=(a == ND - 1))
                    i.then_inc(aux_full, 1)
                    for t in range(NT):
                        for a in range(ND):
                            i = nc.tensor.matmul(aux[:, 1, t * NS:(t + 1) * NS], ut[:, a, t * P:(t + 1) * P],
                                                 wx[:, a, R + NS:R + 2 * NS], start=(a == 0), stop=(a == ND - 1))
                    i.then_inc(aux_full, 1)

                def make_z(c):
                    for a in range(ND):
                        pe.wait_ge(aux_free, c * AUXN + (7 + a))
                        nc.tensor.matmul(aux[:, a % 2], wdt[:, a * P:(a + 1) * P], dc[0:R, :],
                                         start=True, stop=True).then_inc(aux_full, 1)

                def make_dut(c):
                    pe.wait_ge(du_ready, c + 1)
                    for t in range(NT):
                        pe.wait_ge(aux_free, c * AUXN + (11 + t))
                        for a in range(ND):
                            i = nc.tensor.transpose(aux[:, t % 2, a * P:(a + 1) * P],
                                                    s1[:, a * CH + t * P:a * CH + (t + 1) * P], ident[:, :])
                        i.then_inc(aux_full, 1)

                make_ut(0)
                project(0)
                make_z(0)
                make_dut(0)
                pe.wait_ge(prep, 3)
                pe.wait_ge(gam_ready, 1)

                def batch(b, more):
                    for h in range(HALVES):
                        c = chunk(b, h)
                        nxt = h + 1 < HALVES or more

                        def spread_b(s):
                            n, a = divmod(s, ND)
                            pe.wait_ge(bs_ready, c * NS + (n + 1))
                            pe.wait_ge(scan_done, c * STEPS + (SCAN0 + s - 1))
                            for t in range(NT):
                                i = nc.tensor.transpose(dbu[:, s % 2, t * P:(t + 1) * P],
                                                        bs[:, n % 2, t, a * P:(a + 1) * P], ident[:, :])
                            i.then_inc(btr_done, 1)

                        def skip():
                            pe.wait_ge(x1_added, c + 1)
                            for t in range(NT):
                                for a in range(ND):
                                    i = nc.tensor.matmul(y[:, t, a * P:(a + 1) * P], ut[:, a, t * P:(t + 1) * P],
                                                         diag_d[:, a], start=(a == 0), stop=False, skip_group_check=True)
                            i.then_inc(skip_done, 1)

                        def gather(s):
                            n, a = divmod(s, ND)
                            pe.wait_ge(prod_done, c * STEPS + (PROD0 + s + 1))
                            for t in range(NT):
                                i = nc.tensor.matmul(y[:, t, a * P:(a + 1) * P], pp[:, s % 2, t * P:(t + 1) * P],
                                                     ident[:, :], is_transpose=True, start=False,
                                                     stop=(s == STEPS - 1), skip_group_check=True)
                            i.then_inc(rtr_done, 1)

                        for s in range(STEPS):
                            spread_b(s)
                            if s == 2:
                                skip()
                            if s >= 2:
                                gather(s - 2)
                            if nxt and s == 14:
                                make_ut(c + 1)
                            if nxt and s == 22:
                                project(c + 1)
                            if nxt and s == 28:
                                make_z(c + 1)
                            if nxt and s == 56:
                                make_dut(c + 1)
                        gather(STEPS - 2)
                        gather(STEPS - 1)
                        pe.wait_ge(rtr_done, c * STEPS + (RTR0 + STEPS))
                        pe.sem_inc(y_done, 1)

                batches(pe, batch)

            @block.vector
            def _(dve):
                def stats(c, h):
                    dve.wait_ge(x_in[h], c * 8 + (16 - 8 * h))
                    if not (isinstance(c, int) and c == 0):
                        dve.wait_ge(u_ready, c)
                    for t in range(NT):
                        i = nc.vector.bn_stats(st6[:, t], xin[:, h, t])
                    i.then_inc(bn_ready, 1)
                    dve.wait_ge(bn_ready, c + 1)
                    carry_wait(c)
                    for t in range(NT):
                        i = nc.vector.bn_aggr(mv[:, t], st6[:, t])
                    i.then_inc(mv_ready, 1)

                def normalise(c, h):
                    dve.wait_ge(rs_ready, c + 1)
                    if not (isinstance(c, int) and c == 0):
                        dve.wait_ge(aux_full, c * AUXN)
                    for t in range(NT):
                        i = nc.vector.tensor_scalar(s1[:, t * D:(t + 1) * D], xin[:, h, t], mv[:, t, 0:1], rs[:, t:t + 1],
                                                    ALU.subtract, ALU.mult)
                    i.then_inc(u_ready, 1)

                def softplus(c, h):
                    z = delta[:, h].rearrange("p a t -> p (a t)")
                    dve.wait_ge(l_ready, c + 1)
                    nc.vector.scalar_tensor_tensor(z, z, 0.0, s2[h], ALU.max, ALU.add).then_inc(dchain, 1)
                    dve.wait_ge(dchain, c * 4 + 1)
                    nc.vector.tensor_scalar(s2[h], s1[:, :], 1.0, 1.0, ALU.add, ALU.subtract).then_inc(dchain, 1)
                    dve.wait_ge(dchain, c * 4 + 2)
                    nc.vector.tensor_tensor(s2[h], s1[:, :], s2[h], ALU.subtract).then_inc(dchain, 1)
                    dve.wait_ge(dchain, c * 4 + 3)
                    nc.vector.tensor_tensor(z, z, s2[h], ALU.add).then_inc(dchain, 1)

                stats(0, 0)
                normalise(0, 0)
                dve.wait_ge(raw_in, 32)
                nc.vector.tensor_reduce(wsum[:, 1:2], w2_raw, AX.X, ALU.add, apply_absolute_value=True).then_inc(abs_done, 1)
                softplus(0, 0)
                dve.wait_ge(prep, 1)
                nc.vector.tensor_scalar(neg_a[:, :, :], neg_a[:, :, :], -1.0, None, ALU.mult).then_inc(prep, 1)
                for a in range(ND):
                    i = nc.vector.tensor_scalar(diag_d[:, a], ident[:, :], dpar[:, a:a + 1], None, ALU.mult)
                i.then_inc(prep, 1)
                dve.wait_ge(gam_psum, 1)
                nc.vector.tensor_scalar(gam[:, :], y[:, 0, 0:2], 1.0 / (D * F), None, ALU.mult).then_inc(gam_ready, 1)
                dve.wait_ge(gam_ready, 1)
                nc.vector.tensor_scalar(thr[:, :], gam[:, :], BIT_EPS, 0.5, ALU.add, ALU.mult).then_inc(gam_ready, 1)
                dve.wait_ge(gam_ready, 2)
                nc.vector.tensor_scalar(nthr[:, :], thr[:, :], -1.0, None, ALU.mult).then_inc(gam_ready, 1)
                dve.wait_ge(gam_ready, 3)
                for k, (raw, w) in enumerate(((w1_raw, w1), (w2_raw, w2))):
                    wf = w[:, :, :].rearrange("p a f -> p (a f)")
                    nc.vector.tensor_scalar(wf, raw, nthr[:, k:k + 1], None, ALU.is_lt).then_inc(gam_ready, 1)
                    dve.wait_ge(gam_ready, 4 + k)
                    nc.vector.scalar_tensor_tensor(wf, raw, thr[:, k:k + 1], wf, ALU.is_gt, ALU.subtract).then_inc(tern_done, 1)
                dve.sem_inc(scan_done, SCAN0)
                dve.sem_inc(x1_added, 1)

                def batch(b, more):
                    for h in range(HALVES):
                        c = chunk(b, h)
                        nxt = h + 1 < HALVES or more

                        def add_x(cc, hx):
                            dve.wait_ge(y_done, cc + 1)
                            for t in range(NT):
                                i = nc.vector.tensor_tensor(xin[:, hx, t], y[:, t], xin[:, hx, t], ALU.add)
                            i.then_inc(x1_added, 1)

                        for s in range(STEPS):
                            if h > 0 and s == 2:
                                add_x(c - 1, h - 1)
                            if nxt and s == 4:
                                stats(c + 1, 1 - h)
                            if nxt and s == 10:
                                normalise(c + 1, 1 - h)
                            if nxt and s == 44:
                                softplus(c + 1, 1 - h)
                            dve.wait_ge(exp_ready, c * STEPS + (s + 1))
                            dve.wait_ge(btr_done, c * STEPS + (BTR0 + s + 1))
                            dve.wait_ge(prod_done, c * STEPS + (s + 1))
                            if h > 0:
                                dve.wait_ge(state_saved, b * STEPS + (s + 1))
                            nc.vector.tensor_tensor_scan(hh[:, s % 4], da[:, s % 4], dbu[:, s % 2],
                                                         hst[:, s:s + 1] if h > 0 else 0.0,
                                                         ALU.mult, ALU.add).then_inc(scan_done, 1)
                    add_x(chunk(b, HALVES - 1), HALVES - 1)

                batches(dve, batch)

        fb = cb[:, 0, :]
        fc = cb[:, 1, :]
        hb = fb.rearrange("p (r f) -> p r f", r=4)[:, 0:2, :]
        xt = fb[:, 2 * F:2 * F + XRING * D].rearrange("p (r d) -> p r d", r=XRING)
        xq = fb[:, 3 * F:3 * F + 2 * D].rearrange("p (r d) -> p r d", r=2)
        hi = fc[:, 0:F].bitcast(F16).rearrange("p (r f) -> p r f", r=2)
        lo = fc[:, F:2 * F].bitcast(F16).rearrange("p (r f) -> p r f", r=2)
        xhi = fc[:, 2 * F:2 * F + D].bitcast(F16).rearrange("p (r d) -> p r d", r=2)
        xlo = fc[:, 3 * F:3 * F + D].bitcast(F16).rearrange("p (r d) -> p r d", r=2)
        tiny = sb("tiny", [P, 4, 24])
        hst6 = sb("hst6", [P, NB, 6])
        xst6 = sb("xst6", [P, 6])
        tb = dbu
        ob = aux

        xt_in = [sem(f"xt_in{k}") for k in range(XRING)]
        out_done = sem("out_done")
        chain = sem("chain")
        pchain = sem("pchain")
        xq_ready = sem("xq_ready")
        hq_ready = sem("hq_ready")
        t_full = sem("t_full")
        hi_done = sem("hi_done")
        lo_done = sem("lo_done")
        z_full = sem("z_full")
        gelu_done = sem("gelu_done")
        o_full = sem("o_full")
        res_done = sem("res_done")
        sx_ready = sem("sx_ready")
        sh_ready = sem("sh_ready")
        xmax_ready = sem("xmax_ready")
        hmax_ready = sem("hmax_ready")
        TPT = 1 + FC // 4
        G = 4
        RES0 = 2
        XM, HM, XA, HA = 0, 5, 10, 12

        with nc.Block() as block:
            def groups(eng, slot):
                with eng.Fori(0, TILES // G - 1) as g:
                    for j in range(G):
                        slot(g * G + j, j, 3)
                for j in range(G):
                    slot(TILES - G + j, j, G - 1 - j)

            @block.sync
            def _(sp):
                for i in range(XRING):
                    sp.dma_start(xt[:, i:i + 1], x1i[:, i:i + 1]).then_inc(xt_in[i], 16)

                def slot(i, j, left):
                    sp.wait_ge(res_done, i + (RES0 + 1))
                    sp.dma_start(oc[:, bass.ds(i, 1)], xt[:, j:j + 1]).then_inc(out_done, 16)
                    if not isinstance(i, int):
                        sp.wait_ge(out_done, i * 16 + 16)
                        sp.dma_start(xt[:, j:j + 1], x1i[:, bass.ds(i + XRING, 1)]).then_inc(xt_in[j], 16)

                groups(sp, slot)
                sp.wait_ge(out_done, 16 * TILES)

            def t_of_x(i):
                return i if isinstance(i, int) and i < 2 else (i - 2) * TPT + 2 + TPT - 1

            def t_of_h(i, k):
                return i * TPT + (2 + k - (isinstance(i, int) and i == TILES - 1))

            def bank_of_h(i, j, k):
                return (j * TPT + k - (isinstance(i, int) and i == TILES - 1)) % 2

            @block.gpsimd
            def _(pool):
                count = [0]

                def link(ins, base):
                    count[0] += 1
                    ins.then_inc(pchain, 1)
                    pool.wait_ge(pchain, base + count[0])

                def scale_x(i, j, base, n):
                    count[0] = n
                    t = tiny[:, j]
                    pool.wait_ge(xmax_ready, i + 1)
                    var, r, q = t[:, XM + 1:XM + 2], t[:, 14:15], t[:, 15:16]
                    link(nc.gpsimd.tensor_tensor(r, var, ln_eps[:, 0:1], ALU.add), base)
                    link(nc.gpsimd.tensor_tensor(r, r, mhalf[:, 0:1], ALU.pow), base)
                    link(nc.gpsimd.tensor_tensor(q, r, r, ALU.mult), base)
                    link(nc.gpsimd.tensor_tensor(q, q, var, ALU.mult), base)
                    link(nc.gpsimd.tensor_tensor(q, q, bit_eps[:, :], ALU.add), base)
                    link(nc.gpsimd.tensor_tensor(q, q, mhalf[:, 0:1], ALU.pow), base)
                    link(nc.gpsimd.tensor_tensor(r, r, q, ALU.mult), base)
                    link(nc.gpsimd.tensor_tensor(r, r, t[:, XM + 2:XM + 3], ALU.mult), base)
                    nc.gpsimd.tensor_tensor(t[:, 16:17], r, gam[:, 0:1], ALU.mult).then_inc(sx_ready, 1)
                    return count[0]

                def scale_h(i, j, base, n):
                    count[0] = n
                    t = tiny[:, j]
                    pool.wait_ge(hmax_ready, i + 1)
                    r = t[:, 17:18]
                    link(nc.gpsimd.tensor_tensor(r, t[:, HM + 1:HM + 2], bit_eps[:, :], ALU.add), base)
                    link(nc.gpsimd.tensor_tensor(r, r, mhalf[:, 0:1], ALU.pow), base)
                    link(nc.gpsimd.tensor_tensor(r, r, t[:, HM + 2:HM + 3], ALU.mult), base)
                    nc.gpsimd.tensor_tensor(t[:, 18:19], r, gam[:, 1:2], ALU.mult).then_inc(sh_ready, 1)
                    return count[0]

                n = 0
                for i in range(3):
                    n = scale_x(i, i, 0, n)
                n0 = scale_h(0, 0, 0, n)

                def slot(i, j, left):
                    base = i * 11 + (n0 - 8 * max(0, 2 - left))
                    n = 0
                    if left > 0:
                        n = scale_h(i + 1, (j + 1) % G, base, n)
                    if left > 2:
                        scale_x(i + 3, (j + 3) % G, base, n)

                groups(pool, slot)

            @block.scalar
            def _(act):
                def gelus(i, j):
                    act.wait_ge(sx_ready, i + 1)
                    for k in range(NB):
                        act.wait_ge(z_full, i * NB + (k + 1))
                        nc.scalar.activation(hb[:, j % 2, k * 512:(k + 1) * 512], y[:, k], ACT.Gelu,
                                             scale=tiny[:, j, 16:17]).then_inc(gelu_done, 1)

                def hi_x(i, j):
                    act.wait_ge(t_full, t_of_x(i) + 1)
                    nc.scalar.activation(xhi[:, j % 2], tb[:, bank_x[i] if isinstance(i, int) and i < 2 else (TPT - 1 + j) % 2],
                                         ACT.Copy).then_inc(hi_done, 1)

                bank_x = {0: 0, 1: 1}
                hi_x(0, 0)
                gelus(0, 0)
                hi_x(1, 1)
                gelus(1, 1)

                def slot(i, j, left):
                    for k in range(FC // 4):
                        act.wait_ge(t_full, t_of_h(i, k) + 1)
                        nc.scalar.activation(hi[:, j % 2, k * 512:(k + 1) * 512], tb[:, bank_of_h(i, j, k)],
                                             ACT.Copy).then_inc(hi_done, 1)
                    if left > 1:
                        act.wait_ge(t_full, t_of_h(i, TPT - 1) + 1)
                        nc.scalar.activation(xhi[:, j % 2], tb[:, bank_of_h(i, j, TPT - 1)], ACT.Copy).then_inc(hi_done, 1)
                        gelus(i + 2, (j + 2) % G)

                groups(act, slot)

            @block.tensor
            def _(pe):
                pe.wait_ge(x1_added, B * HALVES + 1)

                def z(i, j):
                    pe.wait_ge(lo_done, t_of_x(i) + 1)
                    pe.wait_ge(hi_done, t_of_x(i) + 1)
                    for k in range(NB):
                        if not (isinstance(i, int) and i == 0):
                            pe.wait_ge(gelu_done, (i - 1) * NB + (k + 1))
                        for w, part in enumerate((xhi, xlo)):
                            for a in range(ND):
                                m = nc.tensor.matmul(y[:, k], part[:, j % 2, a * P:(a + 1) * P], w1[:, a, k * 512:(k + 1) * 512],
                                                     start=(w == 0 and a == 0), stop=(w == 1 and a == ND - 1))
                        m.then_inc(z_full, 1)

                def transpose_x(i, j, bank):
                    pe.wait_ge(xq_ready, i + 1)
                    for a in range(ND):
                        m = nc.tensor.transpose(tb[:, bank, a * P:(a + 1) * P], xq[:, j % 2, a * P:(a + 1) * P], ident[:, :])
                    m.then_inc(t_full, 1)

                transpose_x(0, 0, 0)
                transpose_x(1, 1, 1)
                z(0, 0)
                z(1, 1)

                def slot(i, j, left):
                    pe.wait_ge(hq_ready, i + 1)
                    for k in range(FC // 4):
                        pe.wait_ge(hi_done, t_of_h(i, k) - 1)
                        pe.wait_ge(lo_done, t_of_h(i, k) - 1)
                        for a in range(4):
                            q = k * 4 + a
                            m = nc.tensor.transpose(tb[:, bank_of_h(i, j, k), a * P:(a + 1) * P],
                                                    hb[:, j % 2, q * P:(q + 1) * P], ident[:, :])
                        m.then_inc(t_full, 1)
                    if left > 1:
                        pe.wait_ge(hi_done, t_of_h(i, TPT - 1) - 1)
                        pe.wait_ge(lo_done, t_of_h(i, TPT - 1) - 1)
                        transpose_x(i + 2, j, bank_of_h(i, j, TPT - 1))
                    pe.wait_ge(res_done, i + (RES0 - 1))
                    for k in range(FC // 4):
                        pe.wait_ge(hi_done, t_of_h(i, k) + 1)
                        pe.wait_ge(lo_done, t_of_h(i, k) + 1)
                        for w, part in enumerate((hi, lo)):
                            for a in range(4):
                                q = k * 4 + a
                                m = nc.tensor.matmul(ob[:, j % 2], part[:, j % 2, q * P:(q + 1) * P], w2[:, q],
                                                     start=(k == 0 and w == 0 and a == 0),
                                                     stop=(k == FC // 4 - 1 and w == 1 and a == 3))
                    m.then_inc(o_full, 1)
                    if left > 1:
                        z(i + 2, j + 2)

                groups(pe, slot)

            @block.vector
            def _(dve):
                count = [0]

                def link(ins, base, aggregate=False):
                    count[0] += 1
                    ins.then_inc(chain, 1)
                    dve.wait_ge(chain, base + count[0])
                    if aggregate:
                        carry_wait(base)

                def quantise_x(i, j, base, n):
                    count[0] = n
                    t = tiny[:, j]
                    dve.wait_ge(xt_in[j], i * 4 + (16 - 4 * j))
                    xs = xt[:, j]
                    q = xq[:, j % 2]
                    link(nc.vector.bn_stats(xst6[:, :], xs), base, True)
                    link(nc.vector.bn_aggr(t[:, XM:XM + 2], xst6[:, :]), base)
                    if not (isinstance(i, int) and i < 2):
                        dve.wait_ge(t_full, t_of_x(i - 2) + 1 if not isinstance(i, int) or i > 3 else t_of_x(i - 2) + 1)
                    link(nc.vector.tensor_scalar(q, xs, t[:, XM:XM + 1], None, ALU.subtract), base)
                    link(nc.vector.tensor_reduce(t[:, XM + 3:XM + 4], q, AX.X, ALU.max, apply_absolute_value=True), base)
                    count[0] += 1
                    nc.vector.tensor_scalar(t[:, XM + 2:XM + 3], t[:, XM + 3:XM + 4], 1.0 / QB, None,
                                            ALU.mult).then_inc(xmax_ready, 1)
                    count[0] -= 1
                    dve.wait_ge(xmax_ready, i + 1)
                    link(nc.vector.reciprocal(t[:, XM + 4:XM + 5], t[:, XM + 2:XM + 3]), base)
                    nc.vector.tensor_scalar(q, q, t[:, XM + 4:XM + 5], QB, ALU.mult, ALU.min).then_inc(xq_ready, 1)
                    return count[0]

                def quantise_h(i, j, base, n):
                    count[0] = n
                    t = tiny[:, j]
                    h = hb[:, j % 2]
                    for k in range(NB):
                        dve.wait_ge(gelu_done, i * NB + (k + 1))
                        ins = nc.vector.bn_stats(hst6[:, k], h[:, k * 512:(k + 1) * 512])
                    link(ins, base, True)
                    link(nc.vector.bn_aggr(t[:, HM:HM + 2], hst6[:, :, :].rearrange("p a s -> p (a s)")), base)
                    link(nc.vector.tensor_scalar(h, h, t[:, HM:HM + 1], None, ALU.subtract), base)
                    link(nc.vector.tensor_reduce(t[:, HM + 3:HM + 4], h, AX.X, ALU.max, apply_absolute_value=True), base)
                    nc.vector.tensor_scalar(t[:, HM + 2:HM + 3], t[:, HM + 3:HM + 4], 1.0 / QB, None,
                                            ALU.mult).then_inc(hmax_ready, 1)
                    dve.wait_ge(hmax_ready, i + 1)
                    link(nc.vector.reciprocal(t[:, HM + 4:HM + 5], t[:, HM + 2:HM + 3]), base)
                    nc.vector.tensor_scalar(h, h, t[:, HM + 4:HM + 5], QB, ALU.mult, ALU.min).then_inc(hq_ready, 1)
                    return count[0]

                def low_part(k, bank, hi_part, lo_part):
                    dve.wait_ge(hi_done, k + 1)
                    nc.vector.scalar_tensor_tensor(lo_part, tb[:, bank], -QB, hi_part, ALU.max, ALU.subtract).then_inc(lo_done, 1)

                n = 0
                dve.sem_inc(res_done, RES0)
                n = quantise_x(0, 0, 0, n)
                n = quantise_x(1, 1, 0, n)
                low_part(0, 0, xhi[:, 0], xlo[:, 0])
                low_part(1, 1, xhi[:, 1], xlo[:, 1])
                n = quantise_x(2, 2, 0, n)
                n0 = quantise_h(0, 0, 0, n)

                def slot(i, j, left):
                    base = i * 10 + (n0 - 5 * max(0, 2 - left))
                    n = 0
                    for k in range(FC // 4):
                        low_part(t_of_h(i, k), bank_of_h(i, j, k), hi[:, j % 2, k * 512:(k + 1) * 512],
                                 lo[:, j % 2, k * 512:(k + 1) * 512])
                    if left > 1:
                        low_part(t_of_h(i, TPT - 1), bank_of_h(i, j, TPT - 1), xhi[:, j % 2], xlo[:, j % 2])
                    if left > 0:
                        n = quantise_h(i + 1, (j + 1) % G, base, n)
                    if left > 2:
                        quantise_x(i + 3, (j + 3) % G, base, n)
                    dve.wait_ge(o_full, i + 1)
                    dve.wait_ge(sh_ready, i + 1)
                    nc.vector.scalar_tensor_tensor(xt[:, j], ob[:, j % 2], tiny[:, j, 18:19], xt[:, j],
                                                   ALU.mult, ALU.add).then_inc(res_done, 1)

                groups(dve, slot)


def kernel(L0_attn_x, L0_attn_W_xproj, L0_attn_W_dt, L0_attn_b_dt, L0_attn_A_log, L0_attn_D_param,
           L0_ffn_w_fc, L0_ffn_w_proj):
    import numpy as np
    import concourse.bacc as bacc
    from concourse.bass_utils import run_bass_kernel_spmd as run

    wx = np.asarray(L0_attn_W_xproj)
    ns = np.asarray(L0_attn_A_log).shape[1]
    r = wx.shape[0] - 2 * ns
    wx_t = np.ascontiguousarray(np.concatenate([wx[:r], wx[r + ns:], wx[r:r + ns]], axis=0).T)
    arrays = {
        "x": np.ascontiguousarray(L0_attn_x),
        "wx_t": wx_t,
        "wdt_t": np.ascontiguousarray(np.asarray(L0_attn_W_dt).T),
        "b_dt": np.ascontiguousarray(np.asarray(L0_attn_b_dt).reshape(-1, P).T),
        "a_log": np.ascontiguousarray(np.asarray(L0_attn_A_log).reshape(-1, P, ns).transpose(1, 0, 2)),
        "d_param": np.ascontiguousarray(np.asarray(L0_attn_D_param).reshape(-1, P).T),
        "w1_t": np.ascontiguousarray(np.asarray(L0_ffn_w_fc).T),
        "w2_t": np.ascontiguousarray(np.asarray(L0_ffn_w_proj).T),
    }
    nc = bacc.Bacc("TRN2", target_bir_lowering=False, num_devices=1)
    args = [nc.dram_tensor(f"in_{k}", a.shape, mybir.dt.from_np(a.dtype), kind="ExternalInput").ap()
            for k, a in arrays.items()]
    out = nc.dram_tensor("out", arrays["x"].shape, F32, kind="ExternalOutput").ap()
    build(nc, *args, out)
    result = run(nc, [{f"in_{k}": a for k, a in arrays.items()}], core_ids=[0])
    return result.results[0]["out"]
```

```python
from contextlib import ExitStack

import concourse.bass as bass
from concourse import mybir

ALU = mybir.AluOpType
ACT = mybir.ActivationFunctionType
AX = mybir.AxisListType
F32 = mybir.dt.float32
F16 = mybir.dt.float16

P = 128
LN_EPS = 1e-5
BIT_EPS = 1e-6
QB = 128.0


def build(nc, x, wx_t, wdt_t, b_dt, a_log, d_param, w_pieces, out):
    B, L, D = x.shape
    NS = a_log.shape[2]
    R = wdt_t.shape[0]
    WP, _, F = w_pieces.shape
    ND = D // P
    CH = 512
    NT = CH // P
    HALVES = L // CH
    STEPS = NS * ND
    FC = F // P
    NB = F // 512
    TILES = B * L // P
    XRING = 4
    CG = 4
    BEHIND = 3
    LAG = 3
    DVE_U, DVE_SOFT, DVE_W = 5, 42, 20
    POOL_RSTD, POOL_DU = 4, 50
    PE_U, PE_DC, PE_B, PE_Z, PE_DU = [8, 10, 12, 14], 18, 20, [24, 26, 28, 30], [55, 57, 59, 61]
    ACT_SOFT = 36

    xc = x.rearrange("b l d -> (b l) d").rearrange("(c a p) d -> p c a d", p=P, a=NT)
    oc = out.rearrange("b l d -> (b l) d").rearrange("(i p) d -> p i d", p=P)
    x1_dram = nc.dram_tensor("x1_dram", (B * L, D), F32).ap()
    x1c = x1_dram.rearrange("(c a p) d -> p c a d", p=P, a=NT)
    x1i = x1_dram.rearrange("(i p) d -> p i d", p=P)
    c_dram = nc.dram_tensor("c_dram", (B * HALVES, NS, CH), F32).ap()

    with ExitStack() as ctx:
        def sb(name, shape, dt=F32):
            return ctx.enter_context(nc.sbuf_tensor(name, shape, dt))

        def ps(name, shape, dt=F32):
            return ctx.enter_context(nc.psum_tensor(name, shape, dt))

        def sem(name):
            return ctx.enter_context(nc.semaphore(name))

        ident = sb("ident", [P, P])
        ones = sb("ones", [P, P])
        diag_d = sb("diag_d", [P, ND, P])
        wx = sb("wx", [P, ND, R + 2 * NS])
        wdt = sb("wdt", [R, D])
        bdt = sb("bdt", [P, ND])
        dpar = sb("dpar", [P, ND])
        neg_a = sb("neg_a", [P, ND, NS])
        w = sb("w", [P, WP, F], F16)
        wsum = sb("wsum", [P, WP])
        gam = sb("gam", [P, 2])
        thr = sb("thr", [P, WP])
        nthr = sb("nthr", [P, WP])
        mhalf = sb("mhalf", [P, 4])
        ln_eps = sb("ln_eps", [P, 4])
        bit_eps = sb("bit_eps", [P, 1])
        inv_f = sb("inv_f", [P, 1])
        gsum = sb("gsum", [P, 2])
        spare = sb("spare", [P, 1])
        xa = sb("xa", [P, NT, D])
        xb = sb("xb", [P, NT, D])
        s1 = sb("s1", [P, NT * D])
        raw = sb("raw", [P, F])
        ut = sb("ut", [P, ND, CH])
        delta = sb("delta", [P, 2, ND, CH])
        dut = sb("dut", [P, 2, NT, D])
        s2 = [dut[:, k].rearrange("p a d -> p (a d)") for k in range(2)]
        dc = sb("dc", [R + NS, CH])
        bt = sb("bt", [P, 2, NT, NS])
        bs = sb("bs", [P, 2, NT, D])
        da = sb("da", [P, 4, CH])
        hh = sb("hh", [P, 4, CH])
        pp = sb("pp", [P, 4, CH])
        hst = sb("hst", [P, STEPS])
        st6 = sb("st6", [P, NT, 6])
        mv = sb("mv", [P, NT, 2])
        rs = sb("rs", [P, NT])
        cb = sb("cb", [P, CG, NS // CG * CH])

        y = ps("y", [P, NT, 512])
        dbu = ps("dbu", [P, 2, 512])
        aux = ps("aux", [P, 2, 512])

        w_in = sem("w_in")
        xa_in = sem("xa_in")
        xb_in = sem("xb_in")
        sum_in = [sem(f"sum_in{k}") for k in range(WP)]
        raw_in = sem("raw_in")
        const_ready = sem("const_ready")
        id_ready = sem("id_ready")
        prep = sem("prep")
        abs_done = [sem(f"abs_done{k}") for k in range(2)]
        gam_psum = sem("gam_psum")
        gam_ready = sem("gam_ready")
        below_done = sem("below_done")
        tern_done = sem("tern_done")
        mv_ready = sem("mv_ready")
        bn_ready = sem("bn_ready")
        ve_ready = sem("ve_ready")
        rs_ready = sem("rs_ready")
        u_ready = sem("u_ready")
        aux_full = sem("aux_full")
        aux_free = sem("aux_free")
        c_stored = sem("c_stored")
        cb_in = [sem(f"cb_in{k}") for k in range(CG)]
        absz_ready = sem("absz_ready")
        e_ready = sem("e_ready")
        l_ready = sem("l_ready")
        dchain = sem("dchain")
        du_ready = sem("du_ready")
        skip_done = sem("skip_done")
        bs_ready = sem("bs_ready")
        btr_done = sem("btr_done")
        exp_ready = sem("exp_ready")
        scan_done = sem("scan_done")
        prod_done = sem("prod_done")
        rtr_done = sem("rtr_done")
        x1_added = sem("x1_added")
        x1_out = sem("x1_out")
        state_saved = sem("state_saved")

        AUXN = 14
        BTR0, SCAN0, PROD0, RTR0, AUX0 = 8, 4, 4, 4, 2

        def chunk(b, h):
            return b * HALVES + h

        def carry_wait(value):
            if not isinstance(value, int):
                nc.vector.tensor_copy(spare[:, :], ones[:, 0:1])

        def batches(eng, batch):
            with eng.Fori(0, B - 1) as b:
                batch(b, True)
            batch(B - 1, False)

        with nc.Block() as block:
            @block.sync
            def _(sp):
                sp.dma_start(xa[:, :, :], xc[:, 0]).then_inc(xa_in, 16)
                sp.dma_start(wx[:, :, :], wx_t.rearrange("(a p) e -> p a e", p=P)).then_inc(w_in, 16)
                sp.dma_start(wdt[:, :], wdt_t).then_inc(w_in, 16)
                sp.dma_start(bdt[:, :], b_dt).then_inc(w_in, 16)
                sp.dma_start(dpar[:, :], d_param).then_inc(w_in, 16)
                sp.dma_start(neg_a[:, :, :], a_log).then_inc(w_in, 16)
                for k in range(WP):
                    if k >= CG:
                        sp.wait_ge(abs_done[0], k - CG + 1)
                    sp.dma_start(cb[:, k % CG, :], w_pieces[k]).then_inc(sum_in[k], 16)
                sp.dma_start(xb[:, :, :], xc[:, 0]).then_inc(xb_in, 16)
                sp.wait_ge(u_ready, 1)
                sp.dma_start(xa[:, :, :], xc[:, 1]).then_inc(xa_in, 16)

                def store_c(c):
                    sp.wait_ge(aux_free, c * AUXN + (AUX0 + 5))
                    sp.dma_start(c_dram[bass.ds(c, 1)].rearrange("o n t -> (o n) t"), dc[R:R + NS, :]).then_inc(c_stored, 16)
                    sp.wait_ge(c_stored, c * 16 + 16)

                def spread_c(c, g):
                    rows = c_dram[bass.ds(c, 1), g * (NS // CG):(g + 1) * (NS // CG), :]
                    sp.dma_start(cb[:, g, :], rows.rearrange("o n t -> (o n t)").partition_broadcast(P)).then_inc(cb_in[g], 16)

                store_c(0)
                sp.wait_ge(abs_done[1], WP - CG)
                for g in range(CG):
                    spread_c(0, g)

                def batch(b, more):
                    for h in range(HALVES):
                        c = chunk(b, h)
                        nxt = h + 1 < HALVES or more
                        sp.wait_ge(tern_done, c * NT + NT)
                        sp.dma_start(raw[:, :], w_pieces[bass.ds(c, 1)].rearrange("o p f -> (o p) f")).then_inc(raw_in, 16)
                        if more:
                            sp.wait_ge(u_ready, c + 2)
                            sp.dma_start(xa[:, :, :], xc[:, bass.ds(c + 2, 1)]).then_inc(xa_in, 16)
                        if nxt:
                            store_c(c + 1)
                            for g in range(CG):
                                sp.wait_ge(prod_done, c * STEPS + (PROD0 + (g + 1) * STEPS // CG))
                                spread_c(c + 1, g)
                        sp.wait_ge(x1_added, c + 2)
                        sp.dma_start(x1c[:, bass.ds(c, 1)], xb[:, :, :]).then_inc(x1_out, 16)
                        if nxt:
                            sp.wait_ge(x1_out, c * 16 + 16)
                            sp.dma_start(xb[:, :, :], xc[:, bass.ds(c + 1, 1)]).then_inc(xb_in, 16)

                batches(sp, batch)
                sp.wait_ge(x1_out, 16 * B * HALVES)

            @block.gpsimd
            def _(pool):
                nc.gpsimd.memset(ident[:, :], 0.0).then_inc(id_ready, 1)
                nc.gpsimd.memset(ones[:, :], 1.0).then_inc(id_ready, 1)
                nc.gpsimd.memset(mhalf[:, :], -0.5).then_inc(const_ready, 1)
                nc.gpsimd.memset(ln_eps[:, :], LN_EPS).then_inc(const_ready, 1)
                nc.gpsimd.memset(bit_eps[:, :], BIT_EPS).then_inc(const_ready, 1)
                nc.gpsimd.memset(inv_f[:, :], 1.0 / F).then_inc(const_ready, 1)
                pool.wait_ge(id_ready, 2)
                nc.gpsimd.affine_select(out=ident[:, :], in_=ident[:, :], compare_op=ALU.not_equal, fill=1.0,
                                        base=0, pattern=[[-1, P]], channel_multiplier=1).then_inc(id_ready, 1)
                pool.wait_ge(const_ready, 4)

                def rstd(c):
                    pool.wait_ge(mv_ready, c + 1)
                    nc.gpsimd.tensor_tensor(rs[:, :], mv[:, :, 1], ln_eps[:, :], ALU.add).then_inc(ve_ready, 1)
                    pool.wait_ge(ve_ready, c + 1)
                    nc.gpsimd.tensor_tensor(rs[:, :], rs[:, :], mhalf[:, :], ALU.pow).then_inc(rs_ready, 1)

                def du(c, h, a):
                    pool.wait_ge(dchain, c * 16 + (13 + a))
                    nc.gpsimd.tensor_tensor(s1[:, a * CH:(a + 1) * CH], delta[:, h, a], ut[:, a], ALU.mult).then_inc(du_ready, 1)

                rstd(0)
                for a in range(ND):
                    du(0, 0, a)
                pool.sem_inc(prod_done, PROD0)

                def batch(b, more):
                    for h in range(HALVES):
                        c = chunk(b, h)
                        nxt = h + 1 < HALVES or more
                        for s in range(STEPS):
                            if nxt and s == POOL_RSTD:
                                rstd(c + 1)
                            if nxt and POOL_DU <= s < POOL_DU + ND:
                                du(c + 1, 1 - h, s - POOL_DU)
                            n = s // ND
                            per = NS // CG
                            if s % (ND * per) == 0:
                                pool.wait_ge(cb_in[n // per], c * 16 + 16)
                            pool.wait_ge(scan_done, c * STEPS + (SCAN0 + s + 1))
                            pool.wait_ge(rtr_done, c * STEPS + (s + 1))
                            nc.gpsimd.tensor_tensor(pp[:, s % 4], hh[:, s % 4], cb[:, n // per, n % per * CH:(n % per + 1) * CH],
                                                    ALU.mult).then_inc(prod_done, 1)

                batches(pool, batch)

            @block.scalar
            def _(act):
                def magnitudes(k):
                    act.wait_ge(sum_in[k], 16)
                    nc.scalar.activation(w[:, k], cb[:, k % CG, :], ACT.Abs, accum_out=wsum[:, k:k + 1]).then_inc(abs_done[1], 1)

                def evac_ut(c, a):
                    act.wait_ge(skip_done, c + 1)
                    act.wait_ge(aux_full, c * AUXN + (a + 1))
                    nc.scalar.activation(ut[:, a], aux[:, a % 2], ACT.Copy).then_inc(aux_free, 1)

                def evac_dc(c):
                    act.wait_ge(aux_full, c * AUXN + 5)
                    if not isinstance(c, int) or c > 0:
                        act.wait_ge(c_stored, c * 16)
                    nc.scalar.activation(dc[:, :], aux[0:R + NS, 0], ACT.Copy).then_inc(aux_free, 1)

                def evac_bt(c, h):
                    act.wait_ge(aux_full, c * AUXN + 6)
                    nc.scalar.activation(bt[:, h], aux[:, 1, 0:NT * NS].rearrange("p (a n) -> p a n", a=NT),
                                         ACT.Copy).then_inc(aux_free, 1)

                def evac_z(c, h, a):
                    act.wait_ge(aux_full, c * AUXN + (7 + a))
                    nc.scalar.activation(delta[:, h, a], aux[:, a % 2], ACT.Identity, bias=bdt[:, a:a + 1]).then_inc(aux_free, 1)

                def softplus_parts(c, h):
                    act.wait_ge(aux_free, c * AUXN + (AUX0 + 10))
                    nc.scalar.activation(s2[h], delta[:, h].rearrange("p a t -> p (a t)"), ACT.Abs).then_inc(absz_ready, 1)
                    act.wait_ge(absz_ready, c + 1)
                    nc.scalar.activation(s1[:, :], s2[h], ACT.Exp, scale=-1.0).then_inc(e_ready, 1)
                    act.wait_ge(e_ready, c + 1)
                    nc.scalar.activation(s2[h], s1[:, :], ACT.Ln, bias=1.0).then_inc(l_ready, 1)

                def evac_dut(c, h, t):
                    act.wait_ge(aux_full, c * AUXN + (11 + t))
                    nc.scalar.activation(dut[:, h, t], aux[:, t % 2], ACT.Copy).then_inc(aux_free, 1)

                act.sem_inc(aux_free, AUX0)
                for a in range(ND):
                    evac_ut(0, a)
                evac_dc(0)
                evac_bt(0, 0)
                for a in range(ND):
                    evac_z(0, 0, a)
                softplus_parts(0, 0)
                act.wait_ge(w_in, 5 * 16)
                nc.scalar.activation(neg_a[:, :, :], neg_a[:, :, :], ACT.Exp).then_inc(prep, 1)
                for k in range(CG, WP):
                    magnitudes(k)
                for t in range(NT):
                    evac_dut(0, 0, t)

                def batch(b, more):
                    for h in range(HALVES):
                        c = chunk(b, h)
                        nxt = h + 1 < HALVES or more
                        act.wait_ge(aux_free, c * AUXN + (AUX0 + AUXN))
                        for s in range(STEPS):
                            n, a = divmod(s, ND)
                            if nxt:
                                k = s - LAG
                                if k in PE_U:
                                    evac_ut(c + 1, PE_U.index(k))
                                if k == PE_DC:
                                    evac_dc(c + 1)
                                if k == PE_B:
                                    evac_bt(c + 1, 1 - h)
                                if k in PE_Z:
                                    evac_z(c + 1, 1 - h, PE_Z.index(k))
                                if s == ACT_SOFT:
                                    softplus_parts(c + 1, 1 - h)
                                if k in PE_DU:
                                    evac_dut(c + 1, 1 - h, PE_DU.index(k))
                            if a == 0:
                                act.wait_ge(btr_done, c * STEPS + (s + BTR0 - 4))
                                for t in range(NT):
                                    i = nc.scalar.activation(bs[:, n % 2, t], dut[:, h, t], ACT.Copy,
                                                             scale=bt[:, h, t, n:n + 1])
                                i.then_inc(bs_ready, 1)
                            act.wait_ge(scan_done, c * STEPS + (s + 1))
                            nc.scalar.activation(da[:, s % 4], delta[:, h, a], ACT.Exp,
                                                 scale=neg_a[:, a, n:n + 1]).then_inc(exp_ready, 1)
                        if nxt:
                            for k in PE_DU:
                                if k + LAG >= STEPS:
                                    evac_dut(c + 1, 1 - h, PE_DU.index(k))

                act.wait_ge(prep, 2)
                batches(act, batch)

            @block.tensor
            def _(pe):
                pe.sem_inc(rtr_done, RTR0)
                pe.sem_inc(btr_done, BTR0)
                pe.sem_inc(skip_done, 1)
                pe.wait_ge(id_ready, 3)

                def make_ut(c, a):
                    pe.wait_ge(u_ready, c + 1)
                    pe.wait_ge(aux_free, c * AUXN + (a + 1))
                    for t in range(NT):
                        i = nc.tensor.transpose(aux[:, a % 2, t * P:(t + 1) * P],
                                                s1[:, t * D + a * P:t * D + (a + 1) * P], ident[:, :])
                    i.then_inc(aux_full, 1)

                def make_dc(c):
                    pe.wait_ge(aux_free, c * AUXN + (AUX0 + 4))
                    for a in range(ND):
                        i = nc.tensor.matmul(aux[0:R + NS, 0], wx[:, a, 0:R + NS], ut[:, a], start=(a == 0), stop=(a == ND - 1))
                    i.then_inc(aux_full, 1)

                def make_bt(c):
                    pe.wait_ge(aux_free, c * AUXN + (AUX0 + 4))
                    for t in range(NT):
                        for a in range(ND):
                            i = nc.tensor.matmul(aux[:, 1, t * NS:(t + 1) * NS], ut[:, a, t * P:(t + 1) * P],
                                                 wx[:, a, R + NS:R + 2 * NS], start=(a == 0), stop=(a == ND - 1))
                    i.then_inc(aux_full, 1)

                def make_z(c, a):
                    pe.wait_ge(aux_free, c * AUXN + (7 + a))
                    nc.tensor.matmul(aux[:, a % 2], wdt[:, a * P:(a + 1) * P], dc[0:R, :],
                                     start=True, stop=True).then_inc(aux_full, 1)

                def make_dut(c, t):
                    pe.wait_ge(du_ready, c * ND + ND)
                    pe.wait_ge(aux_free, c * AUXN + (11 + t))
                    for a in range(ND):
                        i = nc.tensor.transpose(aux[:, t % 2, a * P:(a + 1) * P],
                                                s1[:, a * CH + t * P:a * CH + (t + 1) * P], ident[:, :])
                    i.then_inc(aux_full, 1)

                for a in range(ND):
                    make_ut(0, a)
                pe.wait_ge(w_in, 5 * 16)
                make_dc(0)
                make_bt(0)
                for a in range(ND):
                    make_z(0, a)
                for t in range(NT):
                    make_dut(0, t)
                pe.wait_ge(abs_done[0], CG)
                pe.wait_ge(abs_done[1], WP - CG)
                nc.tensor.matmul(y[:, 0, 0:WP], ones[:, :], wsum[:, :], start=True, stop=True).then_inc(gam_psum, 1)
                pe.wait_ge(prep, 3)
                pe.wait_ge(gam_ready, 1)

                def batch(b, more):
                    for h in range(HALVES):
                        c = chunk(b, h)
                        nxt = h + 1 < HALVES or more

                        def spread_b(s):
                            n, a = divmod(s, ND)
                            pe.wait_ge(bs_ready, c * NS + (n + 1))
                            pe.wait_ge(scan_done, c * STEPS + (SCAN0 + s - 1))
                            for t in range(NT):
                                i = nc.tensor.transpose(dbu[:, s % 2, t * P:(t + 1) * P],
                                                        bs[:, n % 2, t, a * P:(a + 1) * P], ident[:, :])
                            i.then_inc(btr_done, 1)

                        def skip():
                            pe.wait_ge(x1_added, c + 1)
                            for t in range(NT):
                                for a in range(ND):
                                    i = nc.tensor.matmul(y[:, t, a * P:(a + 1) * P], ut[:, a, t * P:(t + 1) * P],
                                                         diag_d[:, a], start=(a == 0), stop=False, skip_group_check=True)
                            i.then_inc(skip_done, 1)

                        def gather(s):
                            n, a = divmod(s, ND)
                            pe.wait_ge(prod_done, c * STEPS + (PROD0 + s + 1))
                            for t in range(NT):
                                i = nc.tensor.matmul(y[:, t, a * P:(a + 1) * P], pp[:, s % 4, t * P:(t + 1) * P],
                                                     ident[:, :], is_transpose=True, start=False,
                                                     stop=(s == STEPS - 1), skip_group_check=True)
                            i.then_inc(rtr_done, 1)

                        for s in range(STEPS):
                            spread_b(s)
                            if s == 2:
                                skip()
                            if s >= BEHIND:
                                gather(s - BEHIND)
                            if nxt:
                                if s in PE_U:
                                    make_ut(c + 1, PE_U.index(s))
                                if s == PE_DC:
                                    make_dc(c + 1)
                                if s == PE_B:
                                    make_bt(c + 1)
                                if s in PE_Z:
                                    make_z(c + 1, PE_Z.index(s))
                                if s in PE_DU:
                                    make_dut(c + 1, PE_DU.index(s))
                        for s in range(STEPS - BEHIND, STEPS):
                            gather(s)

                batches(pe, batch)

            @block.vector
            def _(dve):
                def stats(c, t):
                    if t == 0:
                        dve.wait_ge(xa_in, c * 16 + 16)
                    i = nc.vector.bn_stats(st6[:, t], xa[:, t])
                    if t == NT - 1:
                        i.then_inc(bn_ready, 1)

                def aggregate(c):
                    dve.wait_ge(bn_ready, c + 1)
                    carry_wait(c)
                    for t in range(NT):
                        i = nc.vector.bn_aggr(mv[:, t], st6[:, t])
                    i.then_inc(mv_ready, 1)

                def normalise(c, t):
                    if t == 0:
                        dve.wait_ge(rs_ready, c + 1)
                        if not isinstance(c, int) or c > 0:
                            dve.wait_ge(aux_full, c * AUXN)
                    i = nc.vector.tensor_scalar(s1[:, t * D:(t + 1) * D], xa[:, t], mv[:, t, 0:1], rs[:, t:t + 1],
                                                ALU.subtract, ALU.mult)
                    if t == NT - 1:
                        i.then_inc(u_ready, 1)

                def softplus(c, h, k):
                    op, a = divmod(k, ND)
                    z = delta[:, h, a]
                    e = s1[:, a * CH:(a + 1) * CH]
                    r = s2[h][:, a * CH:(a + 1) * CH]
                    if op == 0:
                        dve.wait_ge(l_ready, c + 1)
                        i = nc.vector.scalar_tensor_tensor(z, z, 0.0, r, ALU.max, ALU.add)
                    else:
                        dve.wait_ge(dchain, c * 16 + (k - ND + 1))
                    if op == 1:
                        i = nc.vector.tensor_scalar(r, e, 1.0, 1.0, ALU.add, ALU.subtract)
                    if op == 2:
                        i = nc.vector.tensor_tensor(r, e, r, ALU.subtract)
                    if op == 3:
                        i = nc.vector.tensor_tensor(z, z, r, ALU.add)
                    i.then_inc(dchain, 1)

                def ternarise(c, k):
                    q, second = divmod(k, 2)
                    if k == 0:
                        dve.wait_ge(raw_in, c * 16 + 16)
                    r = raw[:, q * CH:(q + 1) * CH]
                    o = w[:, bass.ds(c, 1), q * CH:(q + 1) * CH].rearrange("p o f -> p (o f)")
                    if not second:
                        nc.vector.tensor_scalar(o, r, nthr[:, bass.ds(c, 1)], None, ALU.is_lt).then_inc(below_done, 1)
                    else:
                        dve.wait_ge(below_done, c * NT + (q + 1))
                        nc.vector.scalar_tensor_tensor(o, r, thr[:, bass.ds(c, 1)], o, ALU.is_gt,
                                                       ALU.subtract).then_inc(tern_done, 1)

                for t in range(NT):
                    stats(0, t)
                aggregate(0)
                for t in range(NT):
                    normalise(0, t)
                for k in range(CG):
                    dve.wait_ge(sum_in[k], 16)
                    nc.vector.tensor_reduce(wsum[:, k:k + 1], cb[:, k], AX.X, ALU.add,
                                            apply_absolute_value=True).then_inc(abs_done[0], 1)
                for k in range(16):
                    softplus(0, 0, k)
                dve.wait_ge(prep, 1)
                nc.vector.tensor_scalar(neg_a[:, :, :], neg_a[:, :, :], -1.0, None, ALU.mult).then_inc(prep, 1)
                for a in range(ND):
                    i = nc.vector.tensor_scalar(diag_d[:, a], ident[:, :], dpar[:, a:a + 1], None, ALU.mult)
                i.then_inc(prep, 1)
                dve.wait_ge(gam_psum, 1)
                nc.vector.tensor_reduce(gsum[:, :], y[:, 0, 0:WP].rearrange("p (k q) -> p k q", k=2), AX.X,
                                        ALU.add).then_inc(gam_ready, 1)
                dve.wait_ge(gam_ready, 1)
                nc.vector.tensor_scalar(gam[:, :], gsum[:, :], 1.0 / (D * F), None, ALU.mult).then_inc(gam_ready, 1)
                dve.wait_ge(gam_ready, 2)
                for k in range(WP):
                    i = nc.vector.tensor_scalar(thr[:, k:k + 1], gam[:, k // CG:k // CG + 1], BIT_EPS, 0.5, ALU.add, ALU.mult)
                i.then_inc(gam_ready, 1)
                dve.wait_ge(gam_ready, 3)
                nc.vector.tensor_scalar(nthr[:, :], thr[:, :], -1.0, None, ALU.mult).then_inc(gam_ready, 1)
                dve.wait_ge(gam_ready, 4)
                dve.sem_inc(scan_done, SCAN0)
                dve.sem_inc(x1_added, 1)
                dve.sem_inc(tern_done, NT)

                def batch(b, more):
                    for h in range(HALVES):
                        c = chunk(b, h)
                        nxt = h + 1 < HALVES or more

                        def add_x(cc):
                            dve.wait_ge(xb_in, cc * 16 + 16)
                            dve.wait_ge(rtr_done, cc * STEPS + (RTR0 + STEPS))
                            for t in range(NT):
                                i = nc.vector.tensor_tensor(xb[:, t], y[:, t], xb[:, t], ALU.add)
                            i.then_inc(x1_added, 1)

                        if h > 0:
                            dve.wait_ge(state_saved, b * NS + NS)
                        for s in range(STEPS):
                            n, a = divmod(s, ND)
                            if h > 0 and s == 2:
                                add_x(c - 1)
                            if nxt:
                                if s < 2:
                                    stats(c + 1, 2 * s)
                                    stats(c + 1, 2 * s + 1)
                                if s == 3:
                                    aggregate(c + 1)
                                if DVE_U <= s < DVE_U + 2:
                                    normalise(c + 1, 2 * (s - DVE_U))
                                    normalise(c + 1, 2 * (s - DVE_U) + 1)
                                if DVE_SOFT <= s < DVE_SOFT + 8:
                                    softplus(c + 1, 1 - h, 2 * (s - DVE_SOFT))
                                    softplus(c + 1, 1 - h, 2 * (s - DVE_SOFT) + 1)
                            if DVE_W <= s < DVE_W + 8:
                                ternarise(c, s - DVE_W)
                            if h == 0 and a == 0 and n > 0:
                                dve.wait_ge(state_saved, b * NS + n)
                            dve.wait_ge(exp_ready, c * STEPS + (s + 1))
                            dve.wait_ge(btr_done, c * STEPS + (BTR0 + s + 1))
                            dve.wait_ge(prod_done, c * STEPS + (s + 1))
                            nc.vector.tensor_tensor_scan(hh[:, s % 4], da[:, s % 4], dbu[:, s % 2],
                                                         hst[:, s:s + 1] if h > 0 else 0.0,
                                                         ALU.mult, ALU.add).then_inc(scan_done, 1)
                            if h + 1 < HALVES and a == ND - 1:
                                dve.wait_ge(scan_done, c * STEPS + (SCAN0 + s + 1))
                                nc.vector.tensor_copy(hst[:, n * ND:(n + 1) * ND], hh[:, :, CH - 1]).then_inc(state_saved, 1)
                    add_x(chunk(b, HALVES - 1))

                batches(dve, batch)

        cf = cb[:, :, :].rearrange("p g f -> p (g f)")
        hb = cf[:, 0:2 * F].rearrange("p (r f) -> p r f", r=2)
        hi = cf[:, 2 * F:3 * F].bitcast(F16).rearrange("p (r f) -> p r f", r=2)
        lo = cf[:, 3 * F:4 * F].bitcast(F16).rearrange("p (r f) -> p r f", r=2)
        xt = xb
        xaf = xa[:, :, :].rearrange("p a d -> p (a d)")
        xq = xaf[:, 0:2 * D].rearrange("p (r d) -> p r d", r=2)
        xhi = xaf[:, 2 * D:3 * D].bitcast(F16).rearrange("p (r d) -> p r d", r=2)
        xlo = xaf[:, 3 * D:4 * D].bitcast(F16).rearrange("p (r d) -> p r d", r=2)
        squares = raw
        w1 = w[:, 0:ND, :]
        w2 = w[:, ND:WP, :].rearrange("p g (q d) -> p (g q) d", q=4)
        tiny = sb("tiny", [P, 4, 24])
        xst6 = sb("xst6", [P, 6])
        tb = dbu
        ob = aux

        xt_in = [sem(f"xt_in{k}") for k in range(XRING)]
        out_done = sem("out_done")
        chain = sem("chain")
        pchain = sem("pchain")
        xq_ready = sem("xq_ready")
        hq_ready = sem("hq_ready")
        t_full = sem("t_full")
        hi_done = sem("hi_done")
        lo_done = sem("lo_done")
        z_full = sem("z_full")
        gelu_done = sem("gelu_done")
        mean_done = sem("mean_done")
        centred = sem("centred")
        squared = sem("squared")
        o_full = sem("o_full")
        res_done = sem("res_done")
        sx_ready = sem("sx_ready")
        sh_ready = sem("sh_ready")
        xmax_ready = sem("xmax_ready")
        hmax_ready = sem("hmax_ready")
        HT = FC // 4
        TPT = 1 + HT
        G = 4
        AHEAD = 3
        RES0 = 2
        XMEAN, XVAR, XA, XK, XMAX = range(5)
        HSUM, HNEG, HSQ, HA, HK, HMAX = 5, 9, 10, 11, 12, 13
        RX, QX, SX, RH, SH = 14, 15, 16, 17, 18

        def missed(i):
            return max(0, i - (TILES - AHEAD)) if isinstance(i, int) else 0

        def t_of_x(i):
            return i if isinstance(i, int) and i < AHEAD else (i - AHEAD) * TPT + (AHEAD + HT)

        def t_of_h(i, k):
            return i * TPT + (AHEAD + k - missed(i))

        def bank_of_h(i, j, k):
            return (j * TPT + AHEAD + k - missed(i)) % 2

        def bank_of_x(i, j):
            return (j * TPT + AHEAD + HT) % 2

        with nc.Block() as block:
            def groups(eng, slot):
                with eng.Fori(0, TILES // G - 1) as g:
                    for j in range(G):
                        slot(g * G + j, j, G)
                for j in range(G):
                    slot(TILES - G + j, j, G - 1 - j)

            @block.sync
            def _(sp):
                for i in range(XRING):
                    sp.dma_start(xt[:, i:i + 1], x1i[:, i:i + 1]).then_inc(xt_in[i], 16)

                def slot(i, j, left):
                    sp.wait_ge(res_done, i + (RES0 + 1))
                    sp.dma_start(oc[:, bass.ds(i, 1)], xt[:, j:j + 1]).then_inc(out_done, 16)
                    if not isinstance(i, int):
                        sp.wait_ge(out_done, i * 16 + 16)
                        sp.dma_start(xt[:, j:j + 1], x1i[:, bass.ds(i + XRING, 1)]).then_inc(xt_in[j], 16)

                groups(sp, slot)
                sp.wait_ge(out_done, 16 * TILES)

            @block.gpsimd
            def _(pool):
                count = [0]

                def link(ins, base):
                    count[0] += 1
                    ins.then_inc(pchain, 1)
                    pool.wait_ge(pchain, base + count[0])

                def scale_x(i, j, base, n):
                    count[0] = n
                    var, r, q = (tiny[:, j, k:k + 1] for k in (XVAR, RX, QX))
                    pool.wait_ge(xmax_ready, i + 1)
                    link(nc.gpsimd.tensor_tensor(r, var, ln_eps[:, 0:1], ALU.add), base)
                    link(nc.gpsimd.tensor_tensor(r, r, mhalf[:, 0:1], ALU.pow), base)
                    link(nc.gpsimd.tensor_tensor(q, r, r, ALU.mult), base)
                    link(nc.gpsimd.tensor_tensor(q, q, var, ALU.mult), base)
                    link(nc.gpsimd.tensor_tensor(q, q, bit_eps[:, :], ALU.add), base)
                    link(nc.gpsimd.tensor_tensor(q, q, mhalf[:, 0:1], ALU.pow), base)
                    link(nc.gpsimd.tensor_tensor(r, r, q, ALU.mult), base)
                    link(nc.gpsimd.tensor_tensor(r, r, tiny[:, j, XA:XA + 1], ALU.mult), base)
                    nc.gpsimd.tensor_tensor(tiny[:, j, SX:SX + 1], r, gam[:, 0:1], ALU.mult).then_inc(sx_ready, 1)
                    return count[0]

                def scale_h(i, j, base, n):
                    count[0] = n
                    r = tiny[:, j, RH:RH + 1]
                    pool.wait_ge(hmax_ready, i + 1)
                    pool.wait_ge(squared, i + 1)
                    link(nc.gpsimd.tensor_tensor(r, tiny[:, j, HSQ:HSQ + 1], inv_f[:, :], ALU.mult), base)
                    link(nc.gpsimd.tensor_tensor(r, r, bit_eps[:, :], ALU.add), base)
                    link(nc.gpsimd.tensor_tensor(r, r, mhalf[:, 0:1], ALU.pow), base)
                    link(nc.gpsimd.tensor_tensor(r, r, tiny[:, j, HA:HA + 1], ALU.mult), base)
                    nc.gpsimd.tensor_tensor(tiny[:, j, SH:SH + 1], r, gam[:, 1:2], ALU.mult).then_inc(sh_ready, 1)
                    return count[0]

                n = 0
                for i in range(AHEAD):
                    n = scale_x(i, i, 0, n)
                n0 = scale_h(0, 0, 0, n)

                def slot(i, j, left):
                    base = i * 12 + (n0 - 8 * missed(i))
                    n = 0
                    if left > 0:
                        n = scale_h(i + 1, (j + 1) % G, base, n)
                    if left >= AHEAD:
                        scale_x(i + AHEAD, (j + AHEAD) % G, base, n)

                groups(pool, slot)

            @block.scalar
            def _(act):
                def gelu(i, j, k):
                    if k == 0:
                        act.wait_ge(sx_ready, i + 1)
                    act.wait_ge(z_full, i * NB + (k + 1))
                    nc.scalar.activation(hb[:, j % 2, k * 512:(k + 1) * 512], y[:, k], ACT.Gelu, scale=tiny[:, j, SX:SX + 1],
                                         accum_out=tiny[:, j, HSUM + k:HSUM + k + 1]).then_inc(gelu_done, 1)

                def centre(i, j):
                    t = tiny[:, j]
                    act.wait_ge(gelu_done, i * NB + NB)
                    nc.scalar.activation(t[:, 19:19 + NB], t[:, HSUM:HSUM + NB], ACT.Copy, scale=-1.0 / F,
                                         accum_out=t[:, HNEG:HNEG + 1]).then_inc(mean_done, 1)
                    act.wait_ge(mean_done, i + 1)
                    nc.scalar.activation(hb[:, j % 2], hb[:, j % 2], ACT.Identity, bias=t[:, HNEG:HNEG + 1]).then_inc(centred, 1)
                    act.wait_ge(centred, i + 1)
                    if not isinstance(i, int) or i > 0:
                        act.wait_ge(squared, i)
                    nc.scalar.activation(squares[:, :], hb[:, j % 2], ACT.Square, accum_out=t[:, HSQ:HSQ + 1]).then_inc(squared, 1)

                def hi_x(i, j, bank):
                    act.wait_ge(t_full, t_of_x(i) + 1)
                    nc.scalar.activation(xhi[:, j % 2], tb[:, bank], ACT.Copy).then_inc(hi_done, 1)

                def hi_h(i, j, k):
                    act.wait_ge(t_full, t_of_h(i, k) + 1)
                    nc.scalar.activation(hi[:, j % 2, k * 512:(k + 1) * 512], tb[:, bank_of_h(i, j, k)],
                                         ACT.Copy).then_inc(hi_done, 1)

                hi_x(0, 0, 0)
                hi_x(1, 1, 1)
                for k in range(NB):
                    gelu(0, 0, k)
                hi_x(2, 2, 0)
                centre(0, 0)
                for k in range(NB):
                    gelu(1, 1, k)
                centre(1, 1)

                def slot(i, j, left):
                    hi_h(i, j, 0)
                    hi_h(i, j, 1)
                    if left > 1:
                        gelu(i + 2, (j + 2) % G, 0)
                    hi_h(i, j, 2)
                    hi_h(i, j, 3)
                    if left > 1:
                        for k in range(1, NB):
                            gelu(i + 2, (j + 2) % G, k)
                        centre(i + 2, (j + 2) % G)
                    if left >= AHEAD:
                        hi_x(i + AHEAD, j + AHEAD, bank_of_x(i, j))

                groups(act, slot)

            @block.tensor
            def _(pe):
                def z(i, j, k):
                    if k == 0:
                        pe.wait_ge(lo_done, t_of_x(i) + 1)
                        pe.wait_ge(hi_done, t_of_x(i) + 1)
                    if not isinstance(i, int) or i > 0:
                        pe.wait_ge(gelu_done, i * NB + (k + 1 - NB))
                    for v, part in enumerate((xhi, xlo)):
                        for a in range(ND):
                            m = nc.tensor.matmul(y[:, k], part[:, j % 2, a * P:(a + 1) * P], w1[:, a, k * 512:(k + 1) * 512],
                                                 start=(v == 0 and a == 0), stop=(v == 1 and a == ND - 1))
                    m.then_inc(z_full, 1)

                def free_bank(t):
                    pe.wait_ge(hi_done, t - 1)
                    pe.wait_ge(lo_done, t - 1)

                def transpose_x(i, j, bank):
                    pe.wait_ge(xq_ready, i + 1)
                    for a in range(ND):
                        m = nc.tensor.transpose(tb[:, bank, a * P:(a + 1) * P], xq[:, j % 2, a * P:(a + 1) * P], ident[:, :])
                    m.then_inc(t_full, 1)

                def transpose_h(i, j, k):
                    free_bank(t_of_h(i, k))
                    for a in range(4):
                        q = k * 4 + a
                        m = nc.tensor.transpose(tb[:, bank_of_h(i, j, k), a * P:(a + 1) * P],
                                                hb[:, j % 2, q * P:(q + 1) * P], ident[:, :])
                    m.then_inc(t_full, 1)

                def project(i, j, k):
                    pe.wait_ge(hi_done, t_of_h(i, k) + 1)
                    pe.wait_ge(lo_done, t_of_h(i, k) + 1)
                    for v, part in enumerate((hi, lo)):
                        for a in range(4):
                            q = k * 4 + a
                            m = nc.tensor.matmul(ob[:, j % 2], part[:, j % 2, q * P:(q + 1) * P], w2[:, q],
                                                 start=(k == 0 and v == 0 and a == 0), stop=(k == HT - 1 and v == 1 and a == 3))
                    if k == HT - 1:
                        m.then_inc(o_full, 1)

                transpose_x(0, 0, 0)
                transpose_x(1, 1, 1)
                for k in range(NB):
                    z(0, 0, k)
                free_bank(2)
                transpose_x(2, 2, 0)
                for k in range(NB):
                    z(1, 1, k)

                def slot(i, j, left):
                    ahead = left > 1
                    pe.wait_ge(hq_ready, i + 1)
                    transpose_h(i, j, 0)
                    transpose_h(i, j, 1)
                    if ahead:
                        z(i + 2, j + 2, 0)
                    transpose_h(i, j, 2)
                    transpose_h(i, j, 3)
                    if ahead:
                        z(i + 2, j + 2, 1)
                    pe.wait_ge(res_done, i + (RES0 - 1))
                    project(i, j, 0)
                    project(i, j, 1)
                    if ahead:
                        z(i + 2, j + 2, 2)
                        z(i + 2, j + 2, 3)
                    project(i, j, 2)
                    project(i, j, 3)
                    if left >= AHEAD:
                        free_bank(t_of_x(i + AHEAD))
                        transpose_x(i + AHEAD, j + AHEAD, bank_of_x(i, j))

                groups(pe, slot)

            @block.vector
            def _(dve):
                count = [0]

                def link(ins, base, aggregate=False):
                    count[0] += 1
                    ins.then_inc(chain, 1)
                    dve.wait_ge(chain, base + count[0])
                    if aggregate:
                        carry_wait(base)

                def quantise_x(i, j, base, n, freed):
                    count[0] = n
                    t = tiny[:, j]
                    q = xq[:, j % 2]
                    dve.wait_ge(xt_in[j], i * 4 + (16 - 4 * j))
                    link(nc.vector.bn_stats(xst6[:, :], xt[:, j]), base, True)
                    link(nc.vector.bn_aggr(t[:, XMEAN:XMEAN + 2], xst6[:, :]), base)
                    if freed is not None:
                        dve.wait_ge(t_full, freed)
                    link(nc.vector.tensor_scalar(q, xt[:, j], t[:, XMEAN:XMEAN + 1], None, ALU.subtract), base)
                    link(nc.vector.tensor_reduce(t[:, XMAX:XMAX + 1], q, AX.X, ALU.max, apply_absolute_value=True), base)
                    nc.vector.tensor_scalar(t[:, XA:XA + 1], t[:, XMAX:XMAX + 1], 1.0 / QB, None,
                                            ALU.mult).then_inc(xmax_ready, 1)
                    dve.wait_ge(xmax_ready, i + 1)
                    link(nc.vector.reciprocal(t[:, XK:XK + 1], t[:, XA:XA + 1]), base)
                    nc.vector.tensor_scalar(q, q, t[:, XK:XK + 1], QB, ALU.mult, ALU.min).then_inc(xq_ready, 1)
                    return count[0]

                def quantise_h(i, j, base, n):
                    count[0] = n
                    t = tiny[:, j]
                    h = hb[:, j % 2]
                    dve.wait_ge(centred, i + 1)
                    link(nc.vector.tensor_reduce(t[:, HMAX:HMAX + 1], h, AX.X, ALU.max, apply_absolute_value=True), base)
                    nc.vector.tensor_scalar(t[:, HA:HA + 1], t[:, HMAX:HMAX + 1], 1.0 / QB, None,
                                            ALU.mult).then_inc(hmax_ready, 1)
                    dve.wait_ge(hmax_ready, i + 1)
                    link(nc.vector.reciprocal(t[:, HK:HK + 1], t[:, HA:HA + 1]), base)
                    dve.wait_ge(squared, i + 1)
                    nc.vector.tensor_scalar(h, h, t[:, HK:HK + 1], QB, ALU.mult, ALU.min).then_inc(hq_ready, 1)
                    return count[0]

                def low_part(k, bank, hi_part, lo_part):
                    dve.wait_ge(hi_done, k + 1)
                    nc.vector.scalar_tensor_tensor(lo_part, tb[:, bank], -QB, hi_part, ALU.max, ALU.subtract).then_inc(lo_done, 1)

                dve.sem_inc(res_done, RES0)
                n = quantise_x(0, 0, 0, 0, None)
                n = quantise_x(1, 1, 0, n, None)
                low_part(0, 0, xhi[:, 0], xlo[:, 0])
                low_part(1, 1, xhi[:, 1], xlo[:, 1])
                n = quantise_x(2, 2, 0, n, 1)
                low_part(2, 0, xhi[:, 0], xlo[:, 0])
                n0 = quantise_h(0, 0, 0, n)

                def slot(i, j, left):
                    base = i * 7 + (n0 - 5 * missed(i))
                    n = 0
                    for k in range(HT):
                        low_part(t_of_h(i, k), bank_of_h(i, j, k), hi[:, j % 2, k * 512:(k + 1) * 512],
                                 lo[:, j % 2, k * 512:(k + 1) * 512])
                    if left > 0:
                        n = quantise_h(i + 1, (j + 1) % G, base, n)
                    if left >= AHEAD:
                        quantise_x(i + AHEAD, (j + AHEAD) % G, base, n, t_of_h(i, 0) + 1)
                    dve.wait_ge(o_full, i + 1)
                    dve.wait_ge(sh_ready, i + 1)
                    nc.vector.scalar_tensor_tensor(xt[:, j], ob[:, j % 2], tiny[:, j, SH:SH + 1], xt[:, j],
                                                   ALU.mult, ALU.add).then_inc(res_done, 1)
                    if left >= AHEAD:
                        p = (j + AHEAD) % 2
                        low_part(t_of_x(i + AHEAD), bank_of_x(i, j), xhi[:, p], xlo[:, p])

                groups(dve, slot)


def kernel(L0_attn_x, L0_attn_W_xproj, L0_attn_W_dt, L0_attn_b_dt, L0_attn_A_log, L0_attn_D_param,
           L0_ffn_w_fc, L0_ffn_w_proj):
    import numpy as np
    import concourse.bacc as bacc
    from concourse.bass_utils import run_bass_kernel_spmd as run

    wx = np.asarray(L0_attn_W_xproj)
    ns = np.asarray(L0_attn_A_log).shape[1]
    r = wx.shape[0] - 2 * ns
    wx_t = np.ascontiguousarray(np.concatenate([wx[:r], wx[r + ns:], wx[r:r + ns]], axis=0).T)
    arrays = {
        "x": np.ascontiguousarray(L0_attn_x),
        "wx_t": wx_t,
        "wdt_t": np.ascontiguousarray(np.asarray(L0_attn_W_dt).T),
        "b_dt": np.ascontiguousarray(np.asarray(L0_attn_b_dt).reshape(-1, P).T),
        "a_log": np.ascontiguousarray(np.asarray(L0_attn_A_log).reshape(-1, P, ns).transpose(1, 0, 2)),
        "d_param": np.ascontiguousarray(np.asarray(L0_attn_D_param).reshape(-1, P).T),
        "w_pieces": np.ascontiguousarray(np.concatenate([
            np.asarray(L0_ffn_w_fc).T.reshape(-1, P, L0_ffn_w_fc.shape[0]),
            np.asarray(L0_ffn_w_proj).T.reshape(-1, 4, P, L0_ffn_w_proj.shape[0]).transpose(0, 2, 1, 3).reshape(
                -1, P, L0_ffn_w_fc.shape[0])])),
    }
    nc = bacc.Bacc("TRN2", target_bir_lowering=False, num_devices=1)
    args = [nc.dram_tensor(f"in_{k}", a.shape, mybir.dt.from_np(a.dtype), kind="ExternalInput").ap()
            for k, a in arrays.items()]
    out = nc.dram_tensor("out", arrays["x"].shape, F32, kind="ExternalOutput").ap()
    build(nc, *args, out)
    result = run(nc, [{f"in_{k}": a for k, a in arrays.items()}], core_ids=[0])
    return result.results[0]["out"]
```

```python
from contextlib import ExitStack

import concourse.bass as bass
from concourse import mybir

ALU = mybir.AluOpType
ACT = mybir.ActivationFunctionType
AX = mybir.AxisListType
F32 = mybir.dt.float32
F16 = mybir.dt.float16

P = 128
LN_EPS = 1e-5
BIT_EPS = 1e-6
QB = 128.0



def build(nc, x, wx_t, wdt_t, b_dt, a_log, d_param, w_pieces, out):
    B, L, D = x.shape
    NS = a_log.shape[2]
    R = wdt_t.shape[0]
    ONE = R + 2 * NS
    WP, _, F = w_pieces.shape
    ND = D // P
    CH = 512
    NT = CH // P
    HALVES = L // CH
    STEPS = NS * ND
    FC = F // P
    NB = F // 512
    TILES = B * L // P
    XRING = 4
    BS = 3
    DIAG = (8, 12)
    CG = 4
    VP = 6
    BEHIND = 3
    LAG = 4
    POOL_DG = 10
    DVE_ADD, DVE_STATS, DVE_U, DVE_W, DVE_LN, DVE_SKIP = 3, [0, 1, 2, 4], [8, 8, 9, 9], 22, [45, 46, 47, 48], 53
    SOFT_AT = [31, 32, 33, 34, 35, 36, 38, 39, 40, 41, 42, 43] + DVE_LN
    POOL_RSTD, POOL_DU = 6, [45, 47, 49, 51]
    PE_SKIP, PE_U, PE_DC, PE_B, PE_Z, PE_DU = 3, [10, 12, 14, 16], [16, 18, 20, 22], 26, [27, 30, 35, 38], [53, 54, 55, 56]
    ACT_LN = 46

    xc = x.rearrange("b l d -> (b l) d").rearrange("(c a p) d -> p c a d", p=P, a=NT)
    oc = out.rearrange("b l d -> (b l) d").rearrange("(i p) d -> p i d", p=P)
    x1_dram = nc.dram_tensor("x1_dram", (B * L, D), F32).ap()
    x1c = x1_dram.rearrange("(c a p) d -> p c a d", p=P, a=NT)
    x1i = x1_dram.rearrange("(i p) d -> p i d", p=P)
    c_dram = nc.dram_tensor("c_dram", (B * HALVES, NS, CH), F32).ap()

    with ExitStack() as ctx:
        def sb(name, shape, dt=F32):
            return ctx.enter_context(nc.sbuf_tensor(name, shape, dt))

        def ps(name, shape, dt=F32):
            return ctx.enter_context(nc.psum_tensor(name, shape, dt))

        def sem(name):
            return ctx.enter_context(nc.semaphore(name))

        ident = sb("ident", [P, P])
        ones = sb("ones", [P, P])
        wx = sb("wx", [P, ND, ONE])
        wdt = sb("wdt", [P, D])
        dpar = sb("dpar", [P, ND])
        neg_a = sb("neg_a", [P, ND, NS])
        w = sb("w", [P, WP, F], F16)
        wsum = sb("wsum", [P, WP])
        gam = sb("gam", [P, 2])
        thr = sb("thr", [P, WP])
        nthr = sb("nthr", [P, WP])
        mhalf = sb("mhalf", [P, 4])
        ln_eps = sb("ln_eps", [P, 4])
        bit_eps = sb("bit_eps", [P, 1])
        inv_f = sb("inv_f", [P, 1])
        gsum = sb("gsum", [P, 2])
        spare = sb("spare", [P, 1])
        xa = sb("xa", [P, NT, D])
        xb = sb("xb", [P, NT, D])
        s1 = sb("s1", [P, NT * D])
        xt = s1[:, :].rearrange("p (i d) -> p i d", i=XRING)
        raw = sb("raw", [P, F])
        ut = sb("ut", [P, ND, CH])
        delta = sb("delta", [P, 2, ND, CH])
        dut = sb("dut", [P, 2, NT, D])
        s2 = [dut[:, k].rearrange("p a d -> p (a d)") for k in range(2)]
        dc = sb("dc", [P, CH])
        bt = sb("bt", [P, 2, NT, NS])
        bs = sb("bs", [P, BS, NT, D])
        dg = sb("dg", [P, NT, P])
        da = sb("da", [P, 4, CH])
        hh = sb("hh", [P, 4, CH])
        pp = sb("pp", [P, 4, CH])
        hst = sb("hst", [P, STEPS])
        st6 = sb("st6", [P, NT, 6])
        mv = sb("mv", [P, NT, 2])
        rs = sb("rs", [P, NT])
        cb = sb("cb", [P, CG, NS // CG * CH])

        y = ps("y", [P, NT, 512])
        dbu = ps("dbu", [P, 2, 512])
        aux = ps("aux", [P, 2, 512])

        w_in = sem("w_in")
        xa_in = sem("xa_in")
        xb_in = sem("xb_in")
        sum_in = [sem(f"sum_in{k}") for k in range(WP)]
        raw_in = sem("raw_in")
        const_ready = sem("const_ready")
        id_ready = sem("id_ready")
        prep = sem("prep")
        abs_done = [sem(f"abs_done{k}") for k in range(2)]
        gam_psum = sem("gam_psum")
        gam_ready = sem("gam_ready")
        below_done = sem("below_done")
        tern_done = sem("tern_done")
        mv_ready = sem("mv_ready")
        bn_ready = sem("bn_ready")
        ve_ready = sem("ve_ready")
        rs_ready = sem("rs_ready")
        u_ready = sem("u_ready")
        aux_full = sem("aux_full")
        aux_free = sem("aux_free")
        c_stored = sem("c_stored")
        cb_in = [sem(f"cb_in{k}") for k in range(CG)]
        absz_ready = sem("absz_ready")
        ud_ready = sem("ud_ready")
        e_ready = sem("e_ready")
        l_ready = sem("l_ready")
        dchain = sem("dchain")
        du_ready = sem("du_ready")
        skip_done = sem("skip_done")
        bs_ready = sem("bs_ready")
        dg_ready = sem("dg_ready")
        btr_done = sem("btr_done")
        exp_ready = sem("exp_ready")
        scan_done = sem("scan_done")
        prod_done = sem("prod_done")
        rtr_done = sem("rtr_done")
        x1_added = sem("x1_added")
        xt_in = [sem(f"xt_in{k}") for k in range(XRING)]
        x1_out = sem("x1_out")
        state_saved = sem("state_saved")

        AUXN = 14
        AUXF = 10
        BTR0, SCAN0, PROD0, RTR0, AUX0 = 8, 4, 4, 4, 2

        assert HALVES == 2
        LAST = B * HALVES - 1

        def scaled(n):
            return n + 1 - sum(d <= n for d in DIAG)

        def is_first(c):
            return isinstance(c, int) and c == 0

        def has_next(c):
            return not (isinstance(c, int) and c == LAST)

        def carry_wait(value):
            if not isinstance(value, int):
                nc.vector.tensor_copy(spare[:, :], ones[:, 0:1])

        def chunks(eng, chunk):
            chunk(0, 0, 0)
            with eng.Fori(0, B - 1) as b:
                chunk(b * HALVES + 1, 1, b)
                chunk(b * HALVES + 2, 0, b + 1)
            chunk(LAST, 1, B - 1)

        with nc.Block() as block:
            @block.sync
            def _(sp):
                sp.dma_start(xa[:, :, :], xc[:, 0]).then_inc(xa_in, 16)
                sp.dma_start(wx[:, :, :], wx_t.rearrange("(a p) e -> p a e", p=P)).then_inc(w_in, 16)
                sp.dma_start(dpar[:, :], d_param).then_inc(w_in, 16)
                sp.dma_start(neg_a[:, :, :], a_log).then_inc(w_in, 16)
                sp.wait_ge(id_ready, 4)
                sp.dma_start(wdt[0:R, :], wdt_t).then_inc(w_in, 16)
                sp.dma_start(wdt[ONE:ONE + 1, :], b_dt).then_inc(w_in, 16)
                for k in range(WP):
                    if k >= CG:
                        sp.wait_ge(abs_done[0], k - CG + 1)
                    sp.dma_start(cb[:, k % CG, :], w_pieces[k]).then_inc(sum_in[k], 16)
                sp.dma_start(xb[:, :, :], xc[:, 0]).then_inc(xb_in, 16)
                sp.wait_ge(u_ready, 1)
                sp.dma_start(xa[:, :, :], xc[:, 1]).then_inc(xa_in, 16)

                def store_c(c):
                    sp.wait_ge(aux_free, c * AUXF + (AUX0 + 5))
                    sp.dma_start(c_dram[bass.ds(c, 1)].rearrange("o n t -> (o n) t"), dc[R:R + NS, :]).then_inc(c_stored, 16)
                    sp.wait_ge(c_stored, c * 16 + 16)

                def spread_c(c, g):
                    rows = c_dram[bass.ds(c, 1), g * (NS // CG):(g + 1) * (NS // CG), :]
                    sp.dma_start(cb[:, g, :], rows.rearrange("o n t -> (o n t)").partition_broadcast(P)).then_inc(cb_in[g], 16)

                store_c(0)
                sp.wait_ge(abs_done[0], VP)
                sp.wait_ge(abs_done[1], WP - VP)
                for g in range(CG):
                    spread_c(0, g)

                def batch(b, more):
                    for h in range(HALVES):
                        c = b * HALVES + h
                        nxt = h + 1 < HALVES or more
                        sp.wait_ge(tern_done, c * NT + NT)
                        sp.dma_start(raw[:, :], w_pieces[bass.ds(c, 1)].rearrange("o p f -> (o p) f")).then_inc(raw_in, 16)
                        if more:
                            sp.wait_ge(u_ready, c + 2)
                            sp.dma_start(xa[:, :, :], xc[:, bass.ds(c + 2, 1)]).then_inc(xa_in, 16)
                        if nxt:
                            store_c(c + 1)
                            for g in range(CG):
                                sp.wait_ge(prod_done, c * STEPS + (PROD0 + (g + 1) * STEPS // CG))
                                spread_c(c + 1, g)
                        if not has_next(c):
                            sp.wait_ge(aux_full, B * HALVES * AUXN)
                            for i in range(XRING):
                                sp.dma_start(xt[:, i:i + 1], x1i[:, i:i + 1]).then_inc(xt_in[i], 16)
                        sp.wait_ge(x1_added, c * NT + 2 * NT)
                        sp.dma_start(x1c[:, bass.ds(c, 1)], xb[:, :, :]).then_inc(x1_out, 16)
                        if nxt:
                            sp.wait_ge(x1_out, c * 16 + 16)
                            sp.dma_start(xb[:, :, :], xc[:, bass.ds(c + 1, 1)]).then_inc(xb_in, 16)

                with sp.Fori(0, B - 1) as b:
                    batch(b, True)
                batch(B - 1, False)

            @block.gpsimd
            def _(pool):
                nc.gpsimd.memset(ident[:, :], 0.0).then_inc(id_ready, 1)
                nc.gpsimd.memset(ones[:, :], 1.0).then_inc(id_ready, 1)
                nc.gpsimd.memset(dc[:, :], 1.0).then_inc(id_ready, 1)
                nc.gpsimd.memset(wdt[:, :], 0.0).then_inc(id_ready, 1)
                nc.gpsimd.memset(mhalf[:, :], -0.5).then_inc(const_ready, 1)
                nc.gpsimd.memset(ln_eps[:, :], LN_EPS).then_inc(const_ready, 1)
                nc.gpsimd.memset(bit_eps[:, :], BIT_EPS).then_inc(const_ready, 1)
                nc.gpsimd.memset(inv_f[:, :], 1.0 / F).then_inc(const_ready, 1)
                pool.wait_ge(id_ready, 4)
                nc.gpsimd.affine_select(out=ident[:, :], in_=ident[:, :], compare_op=ALU.not_equal, fill=1.0,
                                        base=0, pattern=[[-1, P]], channel_multiplier=1).then_inc(id_ready, 1)
                pool.wait_ge(const_ready, 4)

                def rstd(c):
                    pool.wait_ge(mv_ready, c + 1)
                    nc.gpsimd.tensor_tensor(rs[:, :], mv[:, :, 1], ln_eps[:, :], ALU.add).then_inc(ve_ready, 1)
                    pool.wait_ge(ve_ready, c + 1)
                    nc.gpsimd.tensor_tensor(rs[:, :], rs[:, :], mhalf[:, :], ALU.pow).then_inc(rs_ready, 1)

                def du(c, h, a):
                    pool.wait_ge(dchain, c * 16 + (13 + a))
                    nc.gpsimd.tensor_tensor(s1[:, a * CH:(a + 1) * CH], delta[:, h, a], ut[:, a], ALU.mult).then_inc(du_ready, 1)

                def diagonal(c, h, k):
                    n = DIAG[k]
                    pool.wait_ge(aux_free, c * AUXF + (AUX0 + 6))
                    pool.wait_ge(btr_done, c * STEPS + (BTR0 + (ND * (DIAG[k - 1] + 1) if k else 0)))
                    nc.gpsimd.tensor_tensor(dg[:, :, :], ident[:, :].unsqueeze(1).to_broadcast([P, NT, P]),
                                            bt[:, h, :, n:n + 1].to_broadcast([P, NT, P]), ALU.mult).then_inc(dg_ready, 1)

                rstd(0)
                for a in range(ND // 2):
                    du(0, 0, a)
                pool.sem_inc(prod_done, PROD0)

                def chunk(c, h, b):
                    nxt = has_next(c)
                    for s in range(STEPS):
                        if nxt and s == POOL_RSTD:
                            rstd(c + 1)
                        if nxt and s in POOL_DU:
                            du(c + 1, 1 - h, POOL_DU.index(s))
                        for k, d in enumerate(DIAG):
                            if s == ND * d - POOL_DG:
                                diagonal(c, h, k)
                        n = s // ND
                        per = NS // CG
                        if s % (ND * per) == 0:
                            pool.wait_ge(cb_in[n // per], c * 16 + 16)
                        pool.wait_ge(scan_done, c * STEPS + (SCAN0 + s + 1))
                        pool.wait_ge(rtr_done, c * STEPS + (s + 1))
                        nc.gpsimd.tensor_tensor(pp[:, s % 4], hh[:, s % 4], cb[:, n // per, n % per * CH:(n % per + 1) * CH],
                                                ALU.mult).then_inc(prod_done, 1)

                chunks(pool, chunk)

            @block.scalar
            def _(act):
                def magnitudes(k):
                    act.wait_ge(sum_in[k], 16)
                    nc.scalar.activation(w[:, k], cb[:, k % CG, :], ACT.Abs, accum_out=wsum[:, k:k + 1]).then_inc(abs_done[1], 1)

                def evac_ut(c, a):
                    act.wait_ge(skip_done, c + 1)
                    act.wait_ge(aux_full, c * AUXN + (a + 1))
                    nc.scalar.activation(ut[:, a], aux[:, a % 2], ACT.Copy).then_inc(aux_free, 1)

                def evac_dc(c):
                    act.wait_ge(aux_full, c * AUXN + 5)
                    if not isinstance(c, int) or c > 0:
                        act.wait_ge(c_stored, c * 16)
                    nc.scalar.activation(dc[0:ONE, :], aux[0:ONE, 0], ACT.Copy).then_inc(aux_free, 1)

                def evac_bt(c, h):
                    act.wait_ge(aux_full, c * AUXN + 6)
                    nc.scalar.activation(bt[:, h], aux[:, 1].rearrange("p (a n) -> p a n", a=NT)[:, :, R + NS:ONE],
                                         ACT.Copy).then_inc(aux_free, 1)

                def abs_z(c, h, a):
                    act.wait_ge(aux_full, c * AUXN + (7 + a))
                    nc.scalar.activation(s2[h][:, a * CH:(a + 1) * CH], aux[:, a % 2], ACT.Abs).then_inc(absz_ready, 1)

                def exp_z(c, h, a):
                    act.wait_ge(absz_ready, c * ND + (a + 1))
                    nc.scalar.activation(s1[:, a * CH:(a + 1) * CH], s2[h][:, a * CH:(a + 1) * CH], ACT.Exp,
                                         scale=-1.0).then_inc(e_ready, 1)

                def log_z(c):
                    act.wait_ge(dchain, c * 16 + 11)
                    nc.scalar.activation(s1[:, :], s1[:, :], ACT.Ln, bias=1.0).then_inc(l_ready, 1)

                def scale_b(h, n, t):
                    i = nc.scalar.activation(bs[:, (n + h) % BS, t], dut[:, h, t], ACT.Copy, scale=bt[:, h, t, n:n + 1])
                    if t == NT - 1:
                        i.then_inc(bs_ready, 1)

                def evac_dut(c, h, t):
                    act.wait_ge(aux_full, c * AUXN + (11 + t))
                    nc.scalar.activation(dut[:, h, t], aux[:, t % 2], ACT.Copy).then_inc(aux_free, 1)

                act.sem_inc(aux_free, AUX0)
                for a in range(ND):
                    evac_ut(0, a)
                evac_dc(0)
                evac_bt(0, 0)
                for a in range(ND):
                    abs_z(0, 0, a)
                    exp_z(0, 0, a)
                log_z(0)
                act.wait_ge(w_in, 5 * 16)
                nc.scalar.activation(neg_a[:, :, :], neg_a[:, :, :], ACT.Exp).then_inc(prep, 1)
                for k in range(VP, WP):
                    magnitudes(k)
                for t in range(NT):
                    evac_dut(0, 0, t)
                act.wait_ge(aux_free, AUX0 + AUXF)
                for t in range(NT):
                    scale_b(0, 0, t)

                def chunk(c, h, b):
                    nxt = has_next(c)
                    for s in range(STEPS):
                        n, a = divmod(s, ND)
                        if nxt:
                            k = s - LAG
                            if k in PE_U:
                                evac_ut(c + 1, PE_U.index(k))
                            if k == PE_DC[-1]:
                                evac_dc(c + 1)
                            if k == PE_B:
                                evac_bt(c + 1, 1 - h)
                            if k in PE_Z:
                                abs_z(c + 1, 1 - h, PE_Z.index(k))
                            if k - 1 in PE_Z:
                                exp_z(c + 1, 1 - h, PE_Z.index(k - 1))
                            if s == ACT_LN:
                                log_z(c + 1)
                            if k in PE_DU:
                                evac_dut(c + 1, 1 - h, PE_DU.index(k))
                        act.wait_ge(scan_done, c * STEPS + (s + 1))
                        nc.scalar.activation(da[:, s % 4], delta[:, h, a], ACT.Exp,
                                             scale=neg_a[:, a, n:n + 1]).then_inc(exp_ready, 1)
                        if n + 1 < NS and n + 1 not in DIAG:
                            if a == 0:
                                act.wait_ge(btr_done, c * STEPS + (s + BTR0 - (0 if s == 0 and h == 0 else 4)))
                            scale_b(h, n + 1, a)
                        elif n + 1 == NS and nxt:
                            if a == 0:
                                act.wait_ge(btr_done, c * STEPS + (s + BTR0))
                            act.wait_ge(aux_free, c * AUXF + (AUXF + AUX0 + 7 + a))
                            scale_b(1 - h, 0, a)

                act.wait_ge(prep, 2)
                chunks(act, chunk)

            @block.tensor
            def _(pe):
                pe.sem_inc(rtr_done, RTR0)
                pe.sem_inc(btr_done, BTR0)
                pe.sem_inc(skip_done, 1)
                pe.wait_ge(id_ready, 5)

                def make_ut(c, a):
                    pe.wait_ge(u_ready, c + 1)
                    pe.wait_ge(aux_free, c * AUXF + (a + 1))
                    for t in range(NT):
                        i = nc.tensor.transpose(aux[:, a % 2, t * P:(t + 1) * P],
                                                s1[:, t * D + a * P:t * D + (a + 1) * P], ident[:, :])
                    i.then_inc(aux_full, 1)

                def make_dc(c, a):
                    if a == 0:
                        pe.wait_ge(aux_free, c * AUXF + (AUX0 + 3))
                    if a == ND - 1:
                        pe.wait_ge(aux_free, c * AUXF + (AUX0 + 4))
                    i = nc.tensor.matmul(aux[0:ONE, 0], wx[:, a], ut[:, a], start=(a == 0), stop=(a == ND - 1))
                    if a == ND - 1:
                        i.then_inc(aux_full, 1)

                def make_bt(c):
                    pe.wait_ge(aux_free, c * AUXF + (AUX0 + 5))
                    for t in range(NT):
                        i = nc.tensor.transpose(aux[:, 1, t * P:(t + 1) * P], dc[:, t * P:(t + 1) * P], ident[:, :])
                    i.then_inc(aux_full, 1)

                def make_z(c, a):
                    if a < 2:
                        pe.wait_ge(aux_free, c * AUXF + (AUX0 + 5 + a))
                    else:
                        pe.wait_ge(dchain, c * 16 + 3 * (a - 1))
                    nc.tensor.matmul(aux[:, a % 2], wdt[:, a * P:(a + 1) * P], dc[:, :],
                                     start=True, stop=True).then_inc(aux_full, 1)

                def make_dut(c, t):
                    pe.wait_ge(du_ready, c * ND + ND)
                    if t >= 2:
                        pe.wait_ge(aux_free, c * AUXF + (AUX0 + 5 + t))
                    for a in range(ND):
                        i = nc.tensor.transpose(aux[:, t % 2, a * P:(a + 1) * P],
                                                s1[:, a * CH + t * P:a * CH + (t + 1) * P], ident[:, :])
                    i.then_inc(aux_full, 1)

                for a in range(ND):
                    make_ut(0, a)
                pe.wait_ge(w_in, 5 * 16)
                for a in range(ND):
                    make_dc(0, a)
                make_bt(0)
                for a in range(ND):
                    make_z(0, a)
                for t in range(NT):
                    make_dut(0, t)
                pe.wait_ge(abs_done[0], VP)
                pe.wait_ge(abs_done[1], WP - VP)
                nc.tensor.matmul(y[:, 0, 0:WP], ones[:, :], wsum[:, :], start=True, stop=True).then_inc(gam_psum, 1)
                pe.wait_ge(prep, 2)
                pe.wait_ge(gam_ready, 1)

                def chunk(c, h, b):
                    nxt = has_next(c)

                    def spread_b(s):
                        n, a = divmod(s, ND)
                        if n in DIAG:
                            pe.wait_ge(dg_ready, c * len(DIAG) + (DIAG.index(n) + 1))
                        else:
                            pe.wait_ge(bs_ready, c * scaled(NS - 1) + scaled(n))
                        pe.wait_ge(scan_done, c * STEPS + (SCAN0 + s - 1))
                        for t in range(NT):
                            if n in DIAG:
                                i = nc.tensor.matmul(dbu[:, s % 2, t * P:(t + 1) * P], dut[:, h, t, a * P:(a + 1) * P],
                                                     dg[:, t], start=True, stop=True)
                            else:
                                i = nc.tensor.transpose(dbu[:, s % 2, t * P:(t + 1) * P],
                                                        bs[:, (n + h) % BS, t, a * P:(a + 1) * P], ident[:, :])
                        i.then_inc(btr_done, 1)

                    def skip():
                        pe.wait_ge(ud_ready, c * ND + ND)
                        for t in range(NT):
                            pe.wait_ge(x1_added, c * NT + (t + 1))
                            for a in range(ND):
                                i = nc.tensor.matmul(y[:, t, a * P:(a + 1) * P], ut[:, a, t * P:(t + 1) * P],
                                                     ident[:, :], is_transpose=True, start=(a == 0), stop=False,
                                                     skip_group_check=True)
                        i.then_inc(skip_done, 1)

                    def gather(c, s):
                        n, a = divmod(s, ND)
                        pe.wait_ge(prod_done, c * STEPS + (PROD0 + s + 1))
                        for t in range(NT):
                            i = nc.tensor.matmul(y[:, t, a * P:(a + 1) * P], pp[:, s % 4, t * P:(t + 1) * P],
                                                 ident[:, :], is_transpose=True, start=False,
                                                 stop=(s == STEPS - 1), skip_group_check=True)
                        i.then_inc(rtr_done, 1)

                    for s in range(STEPS):
                        spread_b(s)
                        if s == PE_SKIP:
                            skip()
                        if s >= BEHIND:
                            gather(c, s - BEHIND)
                        elif not is_first(c):
                            gather(c - 1, s - BEHIND + STEPS)
                        if nxt:
                            if s in PE_U:
                                make_ut(c + 1, PE_U.index(s))
                            if s in PE_DC:
                                make_dc(c + 1, PE_DC.index(s))
                            if s == PE_B:
                                make_bt(c + 1)
                            if s in PE_Z:
                                make_z(c + 1, PE_Z.index(s))
                            if s in PE_DU:
                                make_dut(c + 1, PE_DU.index(s))
                    if not nxt:
                        for s in range(STEPS - BEHIND, STEPS):
                            gather(c, s)

                chunks(pe, chunk)

            @block.vector
            def _(dve):
                def stats(c, t):
                    if t == 0:
                        dve.wait_ge(xa_in, c * 16 + 16)
                    i = nc.vector.bn_stats(st6[:, t], xa[:, t])
                    if t == NT - 1:
                        i.then_inc(bn_ready, 1)

                def aggregate(c):
                    dve.wait_ge(bn_ready, c + 1)
                    carry_wait(c)
                    for t in range(NT):
                        i = nc.vector.bn_aggr(mv[:, t], st6[:, t])
                    i.then_inc(mv_ready, 1)

                def normalise(c, t):
                    if t == 0:
                        dve.wait_ge(rs_ready, c + 1)
                        if not isinstance(c, int) or c > 0:
                            dve.wait_ge(aux_full, c * AUXN)
                    i = nc.vector.tensor_scalar(s1[:, t * D:(t + 1) * D], xa[:, t], mv[:, t, 0:1], rs[:, t:t + 1],
                                                ALU.subtract, ALU.mult)
                    if t == NT - 1:
                        i.then_inc(u_ready, 1)

                def softplus(c, h, k):
                    a, op = divmod(k, 3) if k < 3 * ND else (k - 3 * ND, 3)
                    z = delta[:, h, a]
                    e = s1[:, a * CH:(a + 1) * CH]
                    r = s2[h][:, a * CH:(a + 1) * CH]
                    if op == 0:
                        dve.wait_ge(e_ready, c * ND + (a + 1))
                        i = nc.vector.tensor_scalar(r, e, 1.0, 1.0, ALU.add, ALU.subtract)
                    if op == 1:
                        dve.wait_ge(dchain, c * 16 + (3 * a + 1))
                        i = nc.vector.tensor_tensor(r, e, r, ALU.subtract)
                    if op == 2:
                        dve.wait_ge(dchain, c * 16 + (3 * a + 2))
                        i = nc.vector.scalar_tensor_tensor(z, aux[:, a % 2], 0.0, r, ALU.max, ALU.add)
                    if op == 3:
                        dve.wait_ge(dchain, c * 16 + (3 * a + 3))
                        dve.wait_ge(l_ready, c + 1)
                        i = nc.vector.tensor_tensor(z, z, e, ALU.add)
                    i.then_inc(dchain, 1)

                def scale_u(c, a):
                    dve.wait_ge(du_ready, c * ND + (ND if is_first(c) else a + 1))
                    nc.vector.tensor_scalar(ut[:, a], ut[:, a], dpar[:, a:a + 1], None, ALU.mult).then_inc(ud_ready, 1)

                def add_x(c):
                    dve.wait_ge(xb_in, c * 16 + 16)
                    dve.wait_ge(rtr_done, c * STEPS + (RTR0 + STEPS))
                    for t in range(NT):
                        nc.vector.tensor_tensor(xb[:, t], y[:, t], xb[:, t], ALU.add).then_inc(x1_added, 1)

                def ternarise(c, k):
                    q, second = divmod(k, 2)
                    if k == 0:
                        dve.wait_ge(raw_in, c * 16 + 16)
                    r = raw[:, q * CH:(q + 1) * CH]
                    o = w[:, bass.ds(c, 1), q * CH:(q + 1) * CH].rearrange("p o f -> p (o f)")
                    if not second:
                        nc.vector.tensor_scalar(o, r, nthr[:, bass.ds(c, 1)], None, ALU.is_lt).then_inc(below_done, 1)
                    else:
                        dve.wait_ge(below_done, c * NT + (q + 1))
                        nc.vector.scalar_tensor_tensor(o, r, thr[:, bass.ds(c, 1)], o, ALU.is_gt,
                                                       ALU.subtract).then_inc(tern_done, 1)

                for t in range(NT):
                    stats(0, t)
                aggregate(0)
                for t in range(NT):
                    normalise(0, t)
                for k in range(VP):
                    dve.wait_ge(sum_in[k], 16)
                    nc.vector.tensor_reduce(wsum[:, k:k + 1], cb[:, k % CG], AX.X, ALU.add,
                                            apply_absolute_value=True).then_inc(abs_done[0], 1)
                for k in range(16):
                    softplus(0, 0, k)
                for a in range(ND // 2, ND):
                    dve.wait_ge(dchain, 13 + a)
                    nc.vector.tensor_tensor(s1[:, a * CH:(a + 1) * CH], delta[:, 0, a], ut[:, a], ALU.mult).then_inc(du_ready, 1)
                dve.wait_ge(prep, 1)
                nc.vector.tensor_scalar(neg_a[:, :, :], neg_a[:, :, :], -1.0, None, ALU.mult).then_inc(prep, 1)
                for a in range(ND):
                    scale_u(0, a)
                dve.wait_ge(gam_psum, 1)
                nc.vector.tensor_reduce(gsum[:, :], y[:, 0, 0:WP].rearrange("p (k q) -> p k q", k=2), AX.X,
                                        ALU.add).then_inc(gam_ready, 1)
                dve.wait_ge(gam_ready, 1)
                nc.vector.tensor_scalar(gam[:, :], gsum[:, :], 1.0 / (D * F), None, ALU.mult).then_inc(gam_ready, 1)
                dve.wait_ge(gam_ready, 2)
                for k in range(WP):
                    i = nc.vector.tensor_scalar(thr[:, k:k + 1], gam[:, k // CG:k // CG + 1], BIT_EPS, 0.5, ALU.add, ALU.mult)
                i.then_inc(gam_ready, 1)
                dve.wait_ge(gam_ready, 3)
                nc.vector.tensor_scalar(nthr[:, :], thr[:, :], -1.0, None, ALU.mult).then_inc(gam_ready, 1)
                dve.wait_ge(gam_ready, 4)
                dve.sem_inc(scan_done, SCAN0)
                dve.sem_inc(x1_added, NT)
                dve.sem_inc(tern_done, NT)

                def chunk(c, h, b):
                    nxt = has_next(c)

                    if h > 0:
                        dve.wait_ge(state_saved, b * NS + NS)
                    for s in range(STEPS):
                        n, a = divmod(s, ND)
                        if s == DVE_ADD and not is_first(c):
                            add_x(c - 1)
                        if nxt:
                            if s in DVE_STATS:
                                stats(c + 1, DVE_STATS.index(s))
                            if s == DVE_STATS[-1] + 1:
                                aggregate(c + 1)
                            for t, at in enumerate(DVE_U):
                                if s == at:
                                    normalise(c + 1, t)
                            for k, at in enumerate(SOFT_AT):
                                if s == at:
                                    softplus(c + 1, 1 - h, k)
                            if DVE_SKIP <= s < DVE_SKIP + ND:
                                scale_u(c + 1, s - DVE_SKIP)
                        if DVE_W <= s < DVE_W + 8:
                            ternarise(c, s - DVE_W)
                        if h == 0 and a == 0 and n > 0:
                            dve.wait_ge(state_saved, b * NS + n)
                        dve.wait_ge(exp_ready, c * STEPS + (s + 1))
                        dve.wait_ge(btr_done, c * STEPS + (BTR0 + s + 1))
                        dve.wait_ge(prod_done, c * STEPS + (s + 1))
                        nc.vector.tensor_tensor_scan(hh[:, s % 4], da[:, s % 4], dbu[:, s % 2],
                                                     hst[:, s:s + 1] if h > 0 else 0.0,
                                                     ALU.mult, ALU.add).then_inc(scan_done, 1)
                        if h + 1 < HALVES and a == ND - 1:
                            dve.wait_ge(scan_done, c * STEPS + (SCAN0 + s + 1))
                            nc.vector.tensor_copy(hst[:, n * ND:(n + 1) * ND], hh[:, :, CH - 1]).then_inc(state_saved, 1)

                chunks(dve, chunk)
                add_x(LAST)

        cf = cb[:, :, :].rearrange("p g f -> p (g f)")
        hb = cf[:, 0:2 * F].rearrange("p (r f) -> p r f", r=2)
        hi = cf[:, 2 * F:3 * F].bitcast(F16).rearrange("p (r f) -> p r f", r=2)
        lo = cf[:, 3 * F:4 * F].bitcast(F16).rearrange("p (r f) -> p r f", r=2)
        xaf = xa[:, :, :].rearrange("p a d -> p (a d)")
        xq = xaf[:, 0:2 * D].rearrange("p (r d) -> p r d", r=2)
        xhi = xaf[:, 2 * D:3 * D].bitcast(F16).rearrange("p (r d) -> p r d", r=2)
        xlo = xaf[:, 3 * D:4 * D].bitcast(F16).rearrange("p (r d) -> p r d", r=2)
        squares = raw
        w1 = w[:, 0:ND, :]
        w2 = w[:, ND:WP, :].rearrange("p g (q d) -> p (g q) d", q=4)
        tiny = sb("tiny", [P, 4, 24])
        xst6 = sb("xst6", [P, 6])
        tb = dbu
        ob = aux

        out_done = sem("out_done")
        chain = sem("chain")
        pchain = sem("pchain")
        xq_ready = sem("xq_ready")
        hq_ready = sem("hq_ready")
        t_full = sem("t_full")
        hi_done = sem("hi_done")
        lo_done = sem("lo_done")
        z_full = sem("z_full")
        gelu_done = sem("gelu_done")
        mean_done = sem("mean_done")
        centred = sem("centred")
        squared = sem("squared")
        o_full = sem("o_full")
        res_done = sem("res_done")
        sx_ready = sem("sx_ready")
        sh_ready = sem("sh_ready")
        xmax_ready = sem("xmax_ready")
        hmax_ready = sem("hmax_ready")
        HT = FC // 4
        TPT = 1 + HT
        G = 4
        AHEAD = 3
        RES0 = 2
        XMEAN, XVAR, XA, XK, XMAX = range(5)
        HSUM, HNEG, HSQ, HA, HK, HMAX = 5, 9, 10, 11, 12, 13
        RX, QX, SX, RH, SH = 14, 15, 16, 17, 18

        def missed(i):
            return max(0, i - (TILES - AHEAD)) if isinstance(i, int) else 0

        def t_of_x(i):
            return i if isinstance(i, int) and i < AHEAD else (i - AHEAD) * TPT + (AHEAD + HT)

        def t_of_h(i, k):
            return i * TPT + (AHEAD + k - missed(i))

        def bank_of_h(i, j, k):
            return (j * TPT + AHEAD + k - missed(i)) % 2

        def bank_of_x(i, j):
            return (j * TPT + AHEAD + HT) % 2

        with nc.Block() as block:
            def groups(eng, slot):
                with eng.Fori(0, TILES // G - 1) as g:
                    for j in range(G):
                        slot(g * G + j, j, G)
                for j in range(G):
                    slot(TILES - G + j, j, G - 1 - j)

            @block.sync
            def _(sp):
                sp.wait_ge(x1_out, 16 * B * HALVES)

                def slot(i, j, left):
                    sp.wait_ge(res_done, i + (RES0 + 1))
                    sp.dma_start(oc[:, bass.ds(i, 1)], xt[:, j:j + 1]).then_inc(out_done, 16)
                    if not isinstance(i, int):
                        sp.wait_ge(out_done, i * 16 + 16)
                        sp.dma_start(xt[:, j:j + 1], x1i[:, bass.ds(i + XRING, 1)]).then_inc(xt_in[j], 16)

                groups(sp, slot)
                sp.wait_ge(out_done, 16 * TILES)

            @block.gpsimd
            def _(pool):
                count = [0]

                def link(ins, base):
                    count[0] += 1
                    ins.then_inc(pchain, 1)
                    pool.wait_ge(pchain, base + count[0])

                def scale_x(i, j, base, n):
                    count[0] = n
                    var, r, q = (tiny[:, j, k:k + 1] for k in (XVAR, RX, QX))
                    pool.wait_ge(xmax_ready, i + 1)
                    link(nc.gpsimd.tensor_tensor(r, var, ln_eps[:, 0:1], ALU.add), base)
                    link(nc.gpsimd.tensor_tensor(r, r, mhalf[:, 0:1], ALU.pow), base)
                    link(nc.gpsimd.tensor_tensor(q, r, r, ALU.mult), base)
                    link(nc.gpsimd.tensor_tensor(q, q, var, ALU.mult), base)
                    link(nc.gpsimd.tensor_tensor(q, q, bit_eps[:, :], ALU.add), base)
                    link(nc.gpsimd.tensor_tensor(q, q, mhalf[:, 0:1], ALU.pow), base)
                    link(nc.gpsimd.tensor_tensor(r, r, q, ALU.mult), base)
                    link(nc.gpsimd.tensor_tensor(r, r, tiny[:, j, XA:XA + 1], ALU.mult), base)
                    nc.gpsimd.tensor_tensor(tiny[:, j, SX:SX + 1], r, gam[:, 0:1], ALU.mult).then_inc(sx_ready, 1)
                    return count[0]

                def scale_h(i, j, base, n):
                    count[0] = n
                    r = tiny[:, j, RH:RH + 1]
                    pool.wait_ge(hmax_ready, i + 1)
                    pool.wait_ge(squared, i + 1)
                    link(nc.gpsimd.tensor_tensor(r, tiny[:, j, HSQ:HSQ + 1], inv_f[:, :], ALU.mult), base)
                    link(nc.gpsimd.tensor_tensor(r, r, bit_eps[:, :], ALU.add), base)
                    link(nc.gpsimd.tensor_tensor(r, r, mhalf[:, 0:1], ALU.pow), base)
                    link(nc.gpsimd.tensor_tensor(r, r, tiny[:, j, HA:HA + 1], ALU.mult), base)
                    nc.gpsimd.tensor_tensor(tiny[:, j, SH:SH + 1], r, gam[:, 1:2], ALU.mult).then_inc(sh_ready, 1)
                    return count[0]

                n = 0
                for i in range(AHEAD):
                    n = scale_x(i, i, 0, n)
                n0 = scale_h(0, 0, 0, n)

                def slot(i, j, left):
                    base = i * 12 + (n0 - 8 * missed(i))
                    n = 0
                    if left > 0:
                        n = scale_h(i + 1, (j + 1) % G, base, n)
                    if left >= AHEAD:
                        scale_x(i + AHEAD, (j + AHEAD) % G, base, n)

                groups(pool, slot)

            @block.scalar
            def _(act):
                def gelu(i, j, k):
                    if k == 0:
                        act.wait_ge(sx_ready, i + 1)
                    act.wait_ge(z_full, i * NB + (k + 1))
                    nc.scalar.activation(hb[:, j % 2, k * 512:(k + 1) * 512], y[:, k], ACT.Gelu, scale=tiny[:, j, SX:SX + 1],
                                         accum_out=tiny[:, j, HSUM + k:HSUM + k + 1]).then_inc(gelu_done, 1)

                def centre(i, j):
                    t = tiny[:, j]
                    act.wait_ge(gelu_done, i * NB + NB)
                    nc.scalar.activation(t[:, 19:19 + NB], t[:, HSUM:HSUM + NB], ACT.Copy, scale=-1.0 / F,
                                         accum_out=t[:, HNEG:HNEG + 1]).then_inc(mean_done, 1)
                    act.wait_ge(mean_done, i + 1)
                    nc.scalar.activation(hb[:, j % 2], hb[:, j % 2], ACT.Identity, bias=t[:, HNEG:HNEG + 1]).then_inc(centred, 1)

                def square(i, j):
                    t = tiny[:, j]
                    act.wait_ge(centred, i + 1)
                    if not isinstance(i, int) or i > 0:
                        act.wait_ge(squared, i)
                    nc.scalar.activation(squares[:, :], hb[:, j % 2], ACT.Square, accum_out=t[:, HSQ:HSQ + 1]).then_inc(squared, 1)

                def hi_x(i, j, bank):
                    act.wait_ge(t_full, t_of_x(i) + 1)
                    nc.scalar.activation(xhi[:, j % 2], tb[:, bank], ACT.Copy).then_inc(hi_done, 1)

                def hi_h(i, j, k):
                    act.wait_ge(t_full, t_of_h(i, k) + 1)
                    nc.scalar.activation(hi[:, j % 2, k * 512:(k + 1) * 512], tb[:, bank_of_h(i, j, k)],
                                         ACT.Copy).then_inc(hi_done, 1)

                hi_x(0, 0, 0)
                hi_x(1, 1, 1)
                for k in range(NB):
                    gelu(0, 0, k)
                hi_x(2, 2, 0)
                centre(0, 0)
                square(0, 0)
                for k in range(NB):
                    gelu(1, 1, k)
                centre(1, 1)

                def slot(i, j, left):
                    hi_h(i, j, 0)
                    hi_h(i, j, 1)
                    if left > 0:
                        square(i + 1, (j + 1) % G)
                    if left > 1:
                        gelu(i + 2, (j + 2) % G, 0)
                    hi_h(i, j, 2)
                    hi_h(i, j, 3)
                    if left > 1:
                        gelu(i + 2, (j + 2) % G, 1)
                    if left > 1:
                        gelu(i + 2, (j + 2) % G, 2)
                    if left >= AHEAD:
                        hi_x(i + AHEAD, j + AHEAD, bank_of_x(i, j))
                    if left > 1:
                        gelu(i + 2, (j + 2) % G, 3)
                        centre(i + 2, (j + 2) % G)

                groups(act, slot)

            @block.tensor
            def _(pe):
                def z(i, j, k):
                    if k == 0:
                        pe.wait_ge(lo_done, t_of_x(i) + 1)
                        pe.wait_ge(hi_done, t_of_x(i) + 1)
                    if not isinstance(i, int) or i > 0:
                        pe.wait_ge(gelu_done, i * NB + (k + 1 - NB))
                    for v, part in enumerate((xhi, xlo)):
                        for a in range(ND):
                            m = nc.tensor.matmul(y[:, k], part[:, j % 2, a * P:(a + 1) * P], w1[:, a, k * 512:(k + 1) * 512],
                                                 start=(v == 0 and a == 0), stop=(v == 1 and a == ND - 1))
                    m.then_inc(z_full, 1)

                def free_bank(t):
                    pe.wait_ge(hi_done, t - 1)
                    pe.wait_ge(lo_done, t - 1)

                def transpose_x(i, j, bank):
                    pe.wait_ge(xq_ready, i + 1)
                    for a in range(ND):
                        m = nc.tensor.transpose(tb[:, bank, a * P:(a + 1) * P], xq[:, j % 2, a * P:(a + 1) * P], ident[:, :])
                    m.then_inc(t_full, 1)

                def transpose_h(i, j, k):
                    free_bank(t_of_h(i, k))
                    for a in range(4):
                        q = k * 4 + a
                        m = nc.tensor.transpose(tb[:, bank_of_h(i, j, k), a * P:(a + 1) * P],
                                                hb[:, j % 2, q * P:(q + 1) * P], ident[:, :])
                    m.then_inc(t_full, 1)

                def project(i, j, k):
                    pe.wait_ge(hi_done, t_of_h(i, k) + 1)
                    pe.wait_ge(lo_done, t_of_h(i, k) + 1)
                    for v, part in enumerate((hi, lo)):
                        for a in range(4):
                            q = k * 4 + a
                            m = nc.tensor.matmul(ob[:, j % 2], part[:, j % 2, q * P:(q + 1) * P], w2[:, q],
                                                 start=(k == 0 and v == 0 and a == 0), stop=(k == HT - 1 and v == 1 and a == 3))
                    if k == HT - 1:
                        m.then_inc(o_full, 1)

                transpose_x(0, 0, 0)
                transpose_x(1, 1, 1)
                for k in range(NB):
                    z(0, 0, k)
                free_bank(2)
                transpose_x(2, 2, 0)
                for k in range(NB):
                    z(1, 1, k)

                def slot(i, j, left):
                    ahead = left > 1
                    pe.wait_ge(hq_ready, i + 1)
                    transpose_h(i, j, 0)
                    transpose_h(i, j, 1)
                    if ahead:
                        z(i + 2, j + 2, 0)
                    transpose_h(i, j, 2)
                    transpose_h(i, j, 3)
                    if ahead:
                        z(i + 2, j + 2, 1)
                    pe.wait_ge(res_done, i + (RES0 - 1))
                    project(i, j, 0)
                    project(i, j, 1)
                    if ahead:
                        z(i + 2, j + 2, 2)
                    if left >= AHEAD:
                        free_bank(t_of_x(i + AHEAD))
                        transpose_x(i + AHEAD, j + AHEAD, bank_of_x(i, j))
                    if ahead:
                        z(i + 2, j + 2, 3)
                    project(i, j, 2)
                    project(i, j, 3)

                groups(pe, slot)

            @block.vector
            def _(dve):
                count = [0]

                def link(ins, base, aggregate=False):
                    count[0] += 1
                    ins.then_inc(chain, 1)
                    dve.wait_ge(chain, base + count[0])
                    if aggregate:
                        carry_wait(base)

                def quantise_x(i, j, base, n, freed):
                    count[0] = n
                    t = tiny[:, j]
                    q = xq[:, j % 2]
                    dve.wait_ge(xt_in[j], i * 4 + (16 - 4 * j))
                    link(nc.vector.bn_stats(xst6[:, :], xt[:, j]), base, True)
                    link(nc.vector.bn_aggr(t[:, XMEAN:XMEAN + 2], xst6[:, :]), base)
                    if freed is not None:
                        dve.wait_ge(t_full, freed)
                    link(nc.vector.tensor_scalar(q, xt[:, j], t[:, XMEAN:XMEAN + 1], None, ALU.subtract), base)
                    link(nc.vector.tensor_reduce(t[:, XMAX:XMAX + 1], q, AX.X, ALU.max, apply_absolute_value=True), base)
                    nc.vector.tensor_scalar(t[:, XA:XA + 1], t[:, XMAX:XMAX + 1], 1.0 / QB, None,
                                            ALU.mult).then_inc(xmax_ready, 1)
                    dve.wait_ge(xmax_ready, i + 1)
                    link(nc.vector.reciprocal(t[:, XK:XK + 1], t[:, XA:XA + 1]), base)
                    nc.vector.tensor_scalar(q, q, t[:, XK:XK + 1], QB, ALU.mult, ALU.min).then_inc(xq_ready, 1)
                    return count[0]

                def quantise_h(i, j, base, n):
                    count[0] = n
                    t = tiny[:, j]
                    h = hb[:, j % 2]
                    dve.wait_ge(centred, i + 1)
                    link(nc.vector.tensor_reduce(t[:, HMAX:HMAX + 1], h, AX.X, ALU.max, apply_absolute_value=True), base)
                    nc.vector.tensor_scalar(t[:, HA:HA + 1], t[:, HMAX:HMAX + 1], 1.0 / QB, None,
                                            ALU.mult).then_inc(hmax_ready, 1)
                    dve.wait_ge(hmax_ready, i + 1)
                    link(nc.vector.reciprocal(t[:, HK:HK + 1], t[:, HA:HA + 1]), base)
                    dve.wait_ge(squared, i + 1)
                    nc.vector.tensor_scalar(h, h, t[:, HK:HK + 1], QB, ALU.mult, ALU.min).then_inc(hq_ready, 1)
                    return count[0]

                def low_part(k, bank, hi_part, lo_part):
                    dve.wait_ge(hi_done, k + 1)
                    nc.vector.scalar_tensor_tensor(lo_part, tb[:, bank], -QB, hi_part, ALU.max, ALU.subtract).then_inc(lo_done, 1)

                dve.sem_inc(res_done, RES0)
                n = quantise_x(0, 0, 0, 0, None)
                n = quantise_x(1, 1, 0, n, None)
                low_part(0, 0, xhi[:, 0], xlo[:, 0])
                low_part(1, 1, xhi[:, 1], xlo[:, 1])
                n = quantise_x(2, 2, 0, n, 1)
                low_part(2, 0, xhi[:, 0], xlo[:, 0])
                n0 = quantise_h(0, 0, 0, n)

                def slot(i, j, left):
                    base = i * 7 + (n0 - 5 * missed(i))
                    n = 0
                    for k in range(HT):
                        low_part(t_of_h(i, k), bank_of_h(i, j, k), hi[:, j % 2, k * 512:(k + 1) * 512],
                                 lo[:, j % 2, k * 512:(k + 1) * 512])
                    if left >= AHEAD:
                        n = quantise_x(i + AHEAD, (j + AHEAD) % G, base, n, t_of_h(i, 0) + 1)
                    if left > 0:
                        quantise_h(i + 1, (j + 1) % G, base, n)
                    if left >= AHEAD:
                        p = (j + AHEAD) % 2
                        low_part(t_of_x(i + AHEAD), bank_of_x(i, j), xhi[:, p], xlo[:, p])
                    dve.wait_ge(o_full, i + 1)
                    dve.wait_ge(sh_ready, i + 1)
                    nc.vector.scalar_tensor_tensor(xt[:, j], ob[:, j % 2], tiny[:, j, SH:SH + 1], xt[:, j],
                                                   ALU.mult, ALU.add).then_inc(res_done, 1)

                groups(dve, slot)


def kernel(L0_attn_x, L0_attn_W_xproj, L0_attn_W_dt, L0_attn_b_dt, L0_attn_A_log, L0_attn_D_param,
           L0_ffn_w_fc, L0_ffn_w_proj):
    import numpy as np
    import concourse.bacc as bacc
    from concourse.bass_utils import run_bass_kernel_spmd as run

    wx = np.asarray(L0_attn_W_xproj)
    ns = np.asarray(L0_attn_A_log).shape[1]
    r = wx.shape[0] - 2 * ns
    wx_t = np.ascontiguousarray(np.concatenate([wx[:r], wx[r + ns:], wx[r:r + ns]], axis=0).T)
    arrays = {
        "x": np.ascontiguousarray(L0_attn_x),
        "wx_t": wx_t,
        "wdt_t": np.ascontiguousarray(np.asarray(L0_attn_W_dt).T),
        "b_dt": np.ascontiguousarray(np.asarray(L0_attn_b_dt).reshape(1, -1)),
        "a_log": np.ascontiguousarray(np.asarray(L0_attn_A_log).reshape(-1, P, ns).transpose(1, 0, 2)),
        "d_param": np.ascontiguousarray(np.asarray(L0_attn_D_param).reshape(-1, P).T),
        "w_pieces": np.ascontiguousarray(np.concatenate([
            np.asarray(L0_ffn_w_fc).T.reshape(-1, P, L0_ffn_w_fc.shape[0]),
            np.asarray(L0_ffn_w_proj).T.reshape(-1, 4, P, L0_ffn_w_proj.shape[0]).transpose(0, 2, 1, 3).reshape(
                -1, P, L0_ffn_w_fc.shape[0])])),
    }
    nc = bacc.Bacc("TRN2", target_bir_lowering=False, num_devices=1)
    args = [nc.dram_tensor(f"in_{k}", a.shape, mybir.dt.from_np(a.dtype), kind="ExternalInput").ap()
            for k, a in arrays.items()]
    out = nc.dram_tensor("out", arrays["x"].shape, F32, kind="ExternalOutput").ap()
    build(nc, *args, out)
    result = run(nc, [{f"in_{k}": a for k, a in arrays.items()}], core_ids=[0])
    return result.results[0]["out"]
```
